# Optimizing a Trainium2 kernel written in Bass

```python
import numpy as np
import jax
import jax.numpy as jnp

def _softmax(x, axis=-1):
    return jax.nn.softmax(x, axis=axis)

def _gelu(x):
    return jax.nn.gelu(x, approximate=True)

def _silu(x):
    return jax.nn.silu(x)

def _sigmoid(x):
    return jax.nn.sigmoid(x)

def _layernorm(x, axis=-1, eps=1e-05):
    m = jnp.mean(x, axis=axis, keepdims=True)
    v = jnp.var(x, axis=axis, keepdims=True)
    return (x - m) / jnp.sqrt(v + eps)

def _scatter_add(tgt, idx, src, axis=0):
    return tgt.at[idx].add(src)

def _segment_sum(src, seg, n):
    return jax.ops.segment_sum(src, seg, n)
kernel_name = 'mk_conv_seq_d1_conv_nchw512_r2_c1aab3'

def setup_inputs(seed: int=0):
    np.random.seed(seed)
    _w = jnp.asarray

    def _rec_inputs():
        import jax
        import jax.numpy as jnp
        _gk = jax.random.key(seed)
        x = 7.22e-05 + 1 * jax.random.normal(jax.random.fold_in(_gk, 1), (4, 256, 32, 32), jnp.float32)
        return x
    x = _rec_inputs()

    def _L0_conv_setup():
        import jax, jax.numpy as jnp
        import numpy as np
        C = 256
        CQK = C // 8
        key = jax.random.key(seed)
        ks = jax.random.split(key, 7)
        s = 0.02
        x = jax.random.normal(ks[0], (4, C, 32, 32), dtype=jnp.float32)
        Wq = jax.random.normal(ks[1], (CQK, C), dtype=jnp.float32) * s
        bq = jnp.zeros((CQK,), dtype=jnp.float32)
        Wk = jax.random.normal(ks[2], (CQK, C), dtype=jnp.float32) * s
        bk = jnp.zeros((CQK,), dtype=jnp.float32)
        Wv = jax.random.normal(ks[3], (C, C), dtype=jnp.float32) * s
        bv = jnp.zeros((C,), dtype=jnp.float32)
        return {'x': x, 'Wq': Wq, 'bq': bq, 'Wk': Wk, 'bk': bk, 'Wv': Wv, 'bv': bv}
    _L0_conv_all = _L0_conv_setup()
    _L0_conv_in = {k: v for k, v in _L0_conv_all.items() if k in ('Wq', 'bq', 'Wk', 'bk', 'Wv', 'bv')}
    del _L0_conv_all
    return {'x': x, 'L0_conv_Wq': _L0_conv_in['Wq'], 'L0_conv_bq': _L0_conv_in['bq'], 'L0_conv_Wk': _L0_conv_in['Wk'], 'L0_conv_bk': _L0_conv_in['bk'], 'L0_conv_Wv': _L0_conv_in['Wv'], 'L0_conv_bv': _L0_conv_in['bv']}

def reference(x, L0_conv_Wq, L0_conv_bq, L0_conv_Wk, L0_conv_bk, L0_conv_Wv, L0_conv_bv):
    import jax
    import jax.numpy as jnp

    def _L0_conv_ref(x, Wq, bq, Wk, bk, Wv, bv):
        import jax, jax.numpy as jnp
        import numpy as np
        C = 256
        CQK = C // 8
        B, Cc, W, H = x.shape
        N = W * H
        xf = x.reshape(B, Cc, N)
        q = jnp.einsum('oc,bcn->bon', Wq, xf) + bq[None, :, None]
        k = jnp.einsum('oc,bcn->bon', Wk, xf) + bk[None, :, None]
        v = jnp.einsum('oc,bcn->bon', Wv, xf) + bv[None, :, None]
        scores = jnp.einsum('bqi,bqj->bij', q, k)
        attn = jax.nn.softmax(scores, axis=-1)
        out = jnp.einsum('bcj,bij->bci', v, attn)
        return out.reshape(B, Cc, W, H) + x

    def _gn(v, G=32, eps=1e-05):
        B_, C_, H_, W_ = v.shape
        g = v.reshape(B_, G, C_ // G, H_, W_)
        m = jnp.mean(g, axis=(2, 3, 4), keepdims=True)
        s = jnp.var(g, axis=(2, 3, 4), keepdims=True)
        return ((g - m) / jnp.sqrt(s + eps)).reshape(v.shape)

    def _ln_c(v, eps=1e-06):
        m = jnp.mean(v, axis=1, keepdims=True)
        s = jnp.var(v, axis=1, keepdims=True)
        return (v - m) / jnp.sqrt(s + eps)

    def _ln_t(v, eps=1e-05):
        m = jnp.mean(v, axis=-1, keepdims=True)
        s = jnp.var(v, axis=-1, keepdims=True)
        return (v - m) / jnp.sqrt(s + eps)

    def _to_tokens(v):
        B_, C_, H_, W_ = v.shape
        return v.reshape(B_, C_, H_ * W_).transpose(0, 2, 1)

    def _from_tokens(t, like):
        B_, C_, H_, W_ = like.shape
        return t.transpose(0, 2, 1).reshape(B_, C_, H_, W_)
    x = _L0_conv_ref(x, L0_conv_Wq, L0_conv_bq, L0_conv_Wk, L0_conv_bk, L0_conv_Wv, L0_conv_bv)
    return x

_drawn_inputs = setup_inputs


def setup_inputs(seed=0):
    import zlib

    import numpy as np

    out = dict(_drawn_inputs(seed))
    spreads = {'L0_conv_bq': (0.0, 0.8), 'L0_conv_bk': (0.0, 0.8), 'L0_conv_bv': (0.0, 0.1)}
    factors = {'L0_conv_Wq': 4.268, 'L0_conv_Wk': 4.042, 'L0_conv_Wv': 3.241}
    for name, (base, spread) in spreads.items():
        noise = np.random.default_rng([zlib.crc32(name.encode()), seed]).standard_normal(out[name].shape)
        drawn = base * np.exp(spread * noise) if base else spread * noise
        out[name] = jnp.asarray(drawn.astype(out[name].dtype))
    for name, factor in factors.items():
        out[name] = (out[name] * factor).astype(out[name].dtype)
    return out
```

```python
from contextlib import ExitStack

import concourse.bass as bass
from concourse import mybir


def nonlocal_attention(nc, x, wqk_t, bias_qk, wv_t, bv, out):
    fp32 = mybir.dt.float32
    fp32r = mybir.dt.float32r
    ALU = mybir.AluOpType
    ACT = mybir.ActivationFunctionType
    AX = mybir.AxisListType

    P = 128
    BATCH, C, N = x.shape
    CQK = C // 8
    CT = C // P
    HALF = N // 2
    JT = N // P
    TH = JT // 2
    PER = 2 * JT
    RING = 4
    SHIFT = 3 * CQK
    K_A = SHIFT
    K_B = SHIFT + 2
    DMA = 16
    HI, LO = 0, 1

    x_v = x.rearrange("b (t p) n -> b p t n", p=P)
    out_v = out.rearrange("b (t p) n -> b p t n", p=P)

    ctx = ExitStack()
    with ctx:
        def sb(name, shape, dt=fp32):
            return ctx.enter_context(nc.sbuf_tensor(name, shape, dt))

        def sem(name):
            return ctx.enter_context(nc.semaphore(name))

        x_sb = sb("x_sb", [P, BATCH, CT, N])
        x_hi = sb("x_hi", [P, CT, N], fp32r)
        x_lo = sb("x_lo", [P, CT, N], fp32r)
        wqk = sb("wqk", [P, CT, P])
        wqk_hi = sb("wqk_hi", [P, CT, P], fp32r)
        wqk_lo = sb("wqk_lo", [P, CT, P], fp32r)
        wv = sb("wv", [P, CT, C])
        wv_hi = sb("wv_hi", [P, CT, C], fp32r)
        wv_lo = sb("wv_lo", [P, CT, C], fp32r)
        bias = sb("bias", [P, 1])
        lo_rows = sb("lo_rows", [P, 1])
        lo_bias = sb("lo_bias", [P, 1])
        bv_sb = sb("bv_sb", [P, CT])
        eye = sb("eye", [P, P])
        eye_r = sb("eye_r", [P, P], fp32r)
        ones = sb("ones", [P, N])
        qk_cut = sb("qk_cut", [P, N])
        qk_parts = sb("qk_parts", [P, N], fp32r)
        q_a = sb("q_a", [P, N], fp32r)
        k_a = sb("k_a", [P, N], fp32r)
        q_b = sb("q_b", [P, N], fp32r)
        k_b = sb("k_b", [P, N], fp32r)
        v_hi = sb("v_hi", [P, JT, C], fp32r)
        v_lo = sb("v_lo", [P, JT, C], fp32r)
        dump = sb("dump", [P, 2, N])
        negmax = sb("negmax", [P, JT])
        rowsum = sb("rowsum", [P, JT])
        logsum = sb("logsum", [P, JT])
        shift = sb("shift", [P, JT])
        shift_parts = sb("shift_parts", [P, JT, 2], fp32r)
        w_full = sb("w_full", [P, RING, HALF])
        w_hi = sb("w_hi", [P, RING, HALF], fp32r)
        w_lo = sb("w_lo", [P, RING, HALF], fp32r)
        o_sb = sb("o_sb", [P, 2, CT, HALF])

        acc = [ctx.enter_context(nc.psum_tensor(f"acc{c}", [P, HALF], fp32)) for c in range(CT)]
        st = [ctx.enter_context(nc.psum_tensor(f"st{i}", [P, HALF], fp32)) for i in range(2)]
        slot = [ctx.enter_context(nc.psum_tensor(f"slot{i}", [P, N], fp32)) for i in range(2)]

        x0_in = [sem("x0_in0"), sem("x0_in1")]
        x_in = sem("x_in")
        wqk_in = sem("wqk_in")
        wv_in = sem("wv_in")
        small_in = sem("small_in")
        consts = sem("consts")
        eye_made = sem("eye_made")
        wcut = sem("wcut")
        wsplit = sem("wsplit")
        x_cut = sem("x_cut")
        x_split = sem("x_split")
        qk_ready = sem("qk_ready")
        qk_cut_done = sem("qk_cut_done")
        qk_split = sem("qk_split")
        a_in = [sem("a_in0"), sem("a_in1")]
        qb_in = [sem("qb_in0"), sem("qb_in1")]
        kb_in = [sem("kb_in0"), sem("kb_in1")]
        scores_ready = sem("scores_ready")
        negmax_ready = sem("negmax_ready")
        rowsum_ready = sem("rowsum_ready")
        logsum_ready = sem("logsum_ready")
        shift_full = sem("shift_full")
        shift_cut = sem("shift_cut")
        shift_ready = sem("shift_ready")
        row_ready = sem("row_ready")
        row_put = sem("row_put")
        v_ready = sem("v_ready")
        v_cut = sem("v_cut")
        v_split = sem("v_split")
        st_ready = sem("st_ready")
        exp_done = sem("exp_done")
        w_cut = sem("w_cut")
        w_split = sem("w_split")
        av_done = sem("av_done")
        acc_read = sem("acc_read")
        out_sent = [sem("out_sent0"), sem("out_sent1")]
        sp_passed = sem("sp_passed")
        pool_passed = sem("pool_passed")

        PRE = RING

        def cols(h):
            return slice(h * HALF, (h + 1) * HALF)

        block = ctx.enter_context(nc.Block())

        @block.sync
        def _(sp):
            sp.dma_start(wqk[:, :, :], wqk_t.rearrange("(t p) m -> p t m", p=P)).then_inc(wqk_in, DMA)
            for h in range(2):
                sp.dma_start(x_sb[:, 0, :, cols(h)], x_v[0, :, :, cols(h)]).then_inc(x0_in[h], DMA)
            sp.dma_start(wv[:, :, :], wv_t.rearrange("(t p) m -> p t m", p=P)).then_inc(wv_in, DMA)

            def stack(dst, row, src_row, h, done):
                sp.dma_start(dst[row * CQK:(row + 1) * CQK, cols(h)].bitcast(fp32),
                             qk_parts[src_row * CQK:(src_row + 1) * CQK, cols(h)].bitcast(fp32)).then_inc(done, DMA)

            def q_stack(dst, h, done):
                for row, src in enumerate((0, 2, 0)):
                    stack(dst, row, src, h, done)

            def k_stack(dst, h, done):
                for row, src in enumerate((1, 1, 3)):
                    stack(dst, row, src, h, done)

            def wait(done, count):
                sp.wait_ge(done, count)
                sp.sem_inc(sp_passed, 1)

            def stacks_a(b, first):
                for h in range(2):
                    wait(qk_split, 2 * b + h + 1)
                    if h == 0 and not first:
                        wait(scores_ready, JT * b)
                    q_stack(q_a, h, a_in[h])
                    k_stack(k_a, h, a_in[h])

            stacks_a(0, True)
            for h in range(2):
                q_stack(q_b, h, qb_in[h])
                k_stack(k_b, h, kb_in[h])

            def send(b, h):
                wait(acc_read, 2 * (2 * b + h) + 2)
                sp.dma_start(out_v[b, :, :, cols(h)], o_sb[:, h, :, :]).then_inc(out_sent[h], DMA)

            with sp.Fori(0, BATCH - 1) as b:
                stacks_a(b + 1, False)
                wait(st_ready, PER * b + JT)
                q_stack(q_b, 0, qb_in[0])
                send(b, 0)
                wait(st_ready, PER * b + JT + TH)
                k_stack(k_b, 0, kb_in[0])
                wait(st_ready, PER * b + PER)
                k_stack(k_b, 1, kb_in[1])
                q_stack(q_b, 1, qb_in[1])
                send(b, 1)
            send(BATCH - 1, 0)
            send(BATCH - 1, 1)
            for h in range(2):
                sp.wait_ge(out_sent[h], DMA * BATCH)

        @block.gpsimd
        def _(pool):
            pool.dma_start(bias[:, :], bias_qk).then_inc(small_in, DMA)
            pool.dma_start(bv_sb[:, :], bv).then_inc(small_in, DMA)
            nc.gpsimd.memset(eye[:, :], 0.0).then_inc(eye_made, 1)
            pool.wait_ge(eye_made, 1)
            nc.gpsimd.affine_select(out=eye[:, :], in_=eye[:, :], compare_op=ALU.not_equal, fill=1.0,
                                    base=0, pattern=[[-1, P]], channel_multiplier=1).then_inc(eye_made, 1)
            for b in range(1, BATCH):
                pool.dma_start(x_sb[:, b, :, :], x_v[b]).then_inc(x_in, DMA)
                pool.wait_ge(x_in, DMA * b)

            with pool.Fori(0, BATCH - 1) as b:
                for h in range(2):
                    if h == 0:
                        pool.wait_ge(v_ready, 2 * b + 2)
                        pool.sem_inc(pool_passed, 1)
                    nc.gpsimd.tensor_copy(x_hi[:, :, cols(h)], x_sb[:, b + 1, :, cols(h)]).then_inc(x_cut, 1)
                for h in range(2):
                    pool.wait_ge(x_cut, 2 * b + h + 3)
                    pool.sem_inc(pool_passed, 1)
                    nc.gpsimd.tensor_tensor(x_lo[:, :, cols(h)], x_sb[:, b + 1, :, cols(h)],
                                            x_hi[:, :, cols(h)].bitcast(fp32), ALU.subtract).then_inc(x_split, 1)

        @block.scalar
        def _(act):
            act.preload_act_table_set("natural_log_exp_and_others")
            act.wait_ge(wqk_in, DMA)
            nc.scalar.activation(wqk_hi[:, :, :], wqk[:, :, :], ACT.Copy).then_inc(wcut, 1)
            for h in range(2):
                act.wait_ge(x0_in[h], DMA)
                nc.scalar.activation(x_hi[:, :, cols(h)], x_sb[:, 0, :, cols(h)], ACT.Copy).then_inc(x_cut, 1)
            act.wait_ge(wv_in, DMA)
            nc.scalar.activation(wv_hi[:, :, :], wv[:, :, :], ACT.Copy).then_inc(wcut, 1)
            act.wait_ge(eye_made, 2)
            nc.scalar.activation(eye_r[:, :], eye[:, :], ACT.Copy).then_inc(wcut, 1)
            act.wait_ge(consts, 3)
            nc.scalar.activation(k_b[SHIFT:K_B, :], ones[SHIFT:K_B, :], ACT.Copy).then_inc(wcut, 1)

            def cut_qk(b, h, first):
                act.wait_ge(qk_ready, 2 * b + h + 1)
                if first:
                    act.wait_ge(wsplit, 3)
                nc.scalar.activation(qk_cut[:, cols(h)], slot[h][:, 0:HALF], ACT.Identity,
                                     bias=lo_bias[:, :], scale=lo_rows[:, :]).then_inc(qk_cut_done, 1)

            def sum_exp(T, t):
                act.wait_ge(negmax_ready, T + 1)
                nc.scalar.activation(dump[:, t % 2, :], slot[(t + 1) % 2 if t < TH else t % 2][:, :], ACT.Exp,
                                     bias=negmax[:, t:t + 1], accum_out=rowsum[:, t:t + 1]).then_inc(rowsum_ready, 1)

            def log_sums(b, h):
                act.wait_ge(rowsum_ready, JT * b + TH * h + TH)
                nc.scalar.activation(logsum[:, TH * h:TH * h + TH], rowsum[:, TH * h:TH * h + TH],
                                     ACT.Ln).then_inc(logsum_ready, 1)

            def put_rows(b, h):
                act.wait_ge(row_ready, 2 * b + h + 1)
                nc.scalar.activation(q_b[SHIFT:K_B, cols(h)], slot[0][0:2, 0:HALF], ACT.Copy).then_inc(row_put, 1)

            def cut_v(b, g, first):
                act.wait_ge(v_ready, 2 * b + g + 1)
                if not first:
                    act.wait_ge(av_done, PRE + PER * (b - 1) + JT + TH * g + TH)
                nc.scalar.activation(v_hi[:, TH * g:TH * g + TH, :],
                                     slot[1][:, :].rearrange("p (j c) -> p j c", c=C), ACT.Copy).then_inc(v_cut, 1)

            def exp(n, j):
                act.wait_ge(st_ready, n + 1)
                act.wait_ge(w_split, n + 1)
                nc.scalar.activation(w_full[:, j % RING, :], st[j % 2][:, :], ACT.Exp).then_inc(exp_done, 1)

            for h in range(2):
                cut_qk(0, h, True)
            for t in range(TH):
                sum_exp(t, t)
            log_sums(0, 0)
            cut_v(0, 0, True)
            put_rows(0, 0)
            cut_v(0, 1, True)

            def unit(b, h, more):
                n = PER * b + JT * h
                nh = 1 - h
                nb = b + h
                scores = more or h == 0
                for j in range(JT):
                    exp(n + j, j)
                    if j < TH and scores:
                        sum_exp(JT * nb + TH * nh + j, TH * nh + j)
                    if j == TH - 1 and scores:
                        log_sums(nb, nh)
                    if h == 0 and more and j in (TH, TH + 1):
                        cut_qk(b + 1, j - TH, False)
                    if h == 1 and more and j == TH + 1:
                        cut_v(b + 1, 0, False)
                    if j == JT - 2 and scores:
                        put_rows(nb, nh)
                    if h == 1 and more and j == JT - 1:
                        cut_v(b + 1, 1, False)

            with act.Fori(0, BATCH - 1) as b:
                unit(b, 0, True)
                unit(b, 1, True)
            unit(BATCH - 1, 0, False)
            unit(BATCH - 1, 1, False)

        @block.vector
        def _(dve):
            dve.sem_inc(w_split, PRE)
            nc.vector.memset(lo_rows[0:2 * CQK, :], 0.0).then_inc(consts, 1)
            nc.vector.memset(lo_rows[2 * CQK:4 * CQK, :], 1.0).then_inc(consts, 1)
            nc.vector.memset(ones[SHIFT:SHIFT + 32, :], 1.0).then_inc(consts, 1)
            dve.wait_ge(wcut, 1)
            nc.vector.tensor_tensor(wqk_lo[:, :, :], wqk[:, :, :], wqk_hi[:, :, :].bitcast(fp32),
                                    ALU.subtract).then_inc(wsplit, 1)
            for h in range(2):
                dve.wait_ge(x_cut, h + 1)
                nc.vector.tensor_tensor(x_lo[:, :, cols(h)], x_sb[:, 0, :, cols(h)],
                                        x_hi[:, :, cols(h)].bitcast(fp32), ALU.subtract).then_inc(x_split, 1)
            dve.wait_ge(wcut, 2)
            nc.vector.tensor_tensor(wv_lo[:, :, :], wv[:, :, :], wv_hi[:, :, :].bitcast(fp32),
                                    ALU.subtract).then_inc(wsplit, 1)
            dve.wait_ge(small_in, 2 * DMA)
            dve.wait_ge(consts, 2)
            nc.vector.tensor_tensor(lo_bias[:, :], bias[:, :], lo_rows[:, :], ALU.mult).then_inc(wsplit, 1)

            def split_qk(b, h, first):
                dve.wait_ge(qk_cut_done, 2 * b + h + 1)
                if not first:
                    dve.wait_ge(qb_in[h], 3 * DMA * b)
                    dve.wait_ge(kb_in[h], 3 * DMA * b)
                nc.vector.scalar_tensor_tensor(out=qk_parts[:, cols(h)], in0=slot[h][:, 0:HALF], scalar=bias[:, :],
                                               in1=qk_cut[:, cols(h)], op0=ALU.add, op1=ALU.subtract).then_inc(qk_split, 1)

            def row_max(T, t):
                dve.wait_ge(scores_ready, T + 1)
                nc.vector.tensor_reduce(out=negmax[:, t:t + 1], in_=slot[(t + 1) % 2 if t < TH else t % 2][:, :],
                                        op=ALU.max, axis=AX.X, negate=True).then_inc(negmax_ready, 1)

            def shifts(b, h, step):
                part = slice(TH * h, TH * h + TH)
                if step == 0:
                    dve.wait_ge(logsum_ready, 2 * b + h + 1)
                    nc.vector.tensor_tensor(shift[:, part], negmax[:, part], logsum[:, part],
                                            ALU.subtract).then_inc(shift_full, 1)
                elif step == 1:
                    dve.wait_ge(shift_full, 2 * b + h + 1)
                    nc.vector.tensor_copy(shift_parts[:, part, HI], shift[:, part]).then_inc(shift_cut, 1)
                else:
                    dve.wait_ge(shift_cut, 2 * b + h + 1)
                    nc.vector.tensor_tensor(shift_parts[:, part, LO], shift[:, part],
                                            shift_parts[:, part, HI].bitcast(fp32), ALU.subtract).then_inc(shift_ready, 1)

            def split_v(b, g):
                dve.wait_ge(v_cut, 2 * b + g + 1)
                part = slice(TH * g, TH * g + TH)
                nc.vector.tensor_tensor(v_lo[:, part, :], slot[1][:, :].rearrange("p (j c) -> p j c", c=C),
                                        v_hi[:, part, :].bitcast(fp32), ALU.subtract).then_inc(v_split, 1)

            def cut_w(n, j):
                dve.wait_ge(exp_done, n + 1)
                dve.wait_ge(av_done, n + 1)
                nc.vector.tensor_copy(w_hi[:, j % RING, :], w_full[:, j % RING, :]).then_inc(w_cut, 1)

            def split_w(n, j):
                dve.wait_ge(w_cut, n + 1)
                nc.vector.tensor_tensor(w_lo[:, j % RING, :], w_full[:, j % RING, :],
                                        w_hi[:, j % RING, :].bitcast(fp32), ALU.subtract).then_inc(w_split, 1)

            def finish(b, h, c):
                dve.wait_ge(av_done, PRE + PER * b + JT * h + JT)
                if c == 0:
                    dve.wait_ge(out_sent[h], DMA * b)
                nc.vector.scalar_tensor_tensor(out=o_sb[:, h, c, :], in0=acc[c][:, :], scalar=bv_sb[:, c:c + 1],
                                               in1=x_sb[:, b, c, cols(h)], op0=ALU.add, op1=ALU.add).then_inc(acc_read, 1)

            for h in range(2):
                split_qk(0, h, True)
            for t in range(TH):
                row_max(t, t)
            for step in range(3):
                shifts(0, 0, step)
            split_v(0, 0)
            split_v(0, 1)

            def unit(b, h, more):
                n = PER * b + JT * h
                nh = 1 - h
                nb = b + h
                scores = more or h == 0
                for j in range(JT):
                    cut_w(n + j, j)
                    if j < TH and scores:
                        row_max(JT * nb + TH * nh + j, TH * nh + j)
                    split_w(n + j, j)
                    if h == 0 and more and j in (TH, TH + 1):
                        split_qk(b + 1, j - TH, False)
                    if h == 1 and more and j == TH + 1:
                        split_v(b + 1, 0)
                    if TH <= j < TH + 3 and scores:
                        shifts(nb, nh, j - TH)
                for c in range(CT):
                    finish(b, h, c)
                if h == 1 and more:
                    split_v(b + 1, 1)

            with dve.Fori(0, BATCH - 1) as b:
                unit(b, 0, True)
                unit(b, 1, True)
            unit(BATCH - 1, 0, False)
            unit(BATCH - 1, 1, False)

        @block.tensor
        def _(pe):
            pe.sem_inc(av_done, PRE)

            def group(dst, terms):
                for i, (lhs, rhs) in enumerate(terms):
                    last = nc.tensor.matmul(dst, lhs, rhs, start=(i == 0), stop=(i == len(terms) - 1))
                return last

            def project_qk(b, h, first):
                if first:
                    pe.wait_ge(wsplit, 1)
                    pe.wait_ge(x_split, h + 1)
                else:
                    pe.wait_ge(x_split, 2 * b + h + 1)
                    pe.wait_ge(rowsum_ready, JT * (b - 1) + JT - 1 + h)
                terms = [(w[:, c, :], xs[:, c, cols(h)]) for c in range(CT)
                         for w, xs in ((wqk_hi, x_hi), (wqk_lo, x_hi), (wqk_hi, x_lo))]
                group(slot[h][:, 0:HALF], terms).then_inc(qk_ready, 1)

            def scores(T, t):
                dst = slot[(t + 1) % 2 if t < TH else t % 2]
                for h in range(2):
                    last = nc.tensor.matmul(dst[:, cols(h)], q_a[0:K_A, t * P:(t + 1) * P], k_a[0:K_A, cols(h)],
                                            start=True, stop=True)
                last.then_inc(scores_ready, 1)

            def project_v(b, g):
                for jj in range(TH):
                    px = slice((TH * g + jj) * P, (TH * g + jj + 1) * P)
                    terms = [(xs[:, c, px], w[:, c, :]) for c in range(CT)
                             for xs, w in ((x_hi, wv_hi), (x_hi, wv_lo), (x_lo, wv_hi))]
                    last = group(slot[1][:, jj * C:(jj + 1) * C], terms)
                last.then_inc(v_ready, 1)

            def rows(b, h, first):
                pe.wait_ge(shift_ready, 2 * b + h + 1)
                for t in range(TH):
                    last = nc.tensor.matmul(slot[0][0:2, t * P:(t + 1) * P], shift_parts[:, TH * h + t, :], eye_r[:, :],
                                            start=True, stop=True)
                last.then_inc(row_ready, 1)

            def scores_t(b, h, j):
                if j == 0:
                    pe.wait_ge(row_put, 2 * b + h + 1)
                    pe.wait_ge(qb_in[h], 3 * DMA * (b + 1))
                    if h == 0:
                        pe.wait_ge(kb_in[0], 3 * DMA * (b + 1))
                if j == TH and h == 0:
                    pe.wait_ge(kb_in[1], 3 * DMA * (b + 1))
                nc.tensor.matmul(st[j % 2][:, :], k_b[0:K_B, j * P:(j + 1) * P], q_b[0:K_B, cols(h)],
                                 start=True, stop=True).then_inc(st_ready, 1)

            def weigh_v(b, h, j):
                n = PER * b + JT * h + j
                r = j % RING
                if h == 0 and j in (0, TH):
                    pe.wait_ge(v_split, 2 * b + 1 + j // TH)
                pe.wait_ge(w_cut, n + 1)
                for c in range(CT):
                    ch = slice(c * P, (c + 1) * P)
                    for v in (v_hi, v_lo):
                        nc.tensor.matmul(acc[c][:, :], v[:, j, ch], w_hi[:, r, :],
                                         start=(j == 0 and v is v_hi), stop=False)
                pe.wait_ge(w_split, PRE + n + 1)
                for c in range(CT):
                    ch = slice(c * P, (c + 1) * P)
                    last = nc.tensor.matmul(acc[c][:, :], v_hi[:, j, ch], w_lo[:, r, :], start=False, stop=(j == JT - 1))
                last.then_inc(av_done, 1)

            for h in range(2):
                project_qk(0, h, True)
            for h in range(2):
                pe.wait_ge(a_in[h], 6 * DMA)
            pe.wait_ge(qk_split, 2)
            for t in range(TH):
                if t >= 2:
                    pe.wait_ge(rowsum_ready, t - 1)
                scores(t, t)
            pe.wait_ge(wsplit, 2)
            pe.wait_ge(rowsum_ready, TH - 1)
            project_v(0, 0)
            pe.wait_ge(wcut, 4)
            pe.wait_ge(rowsum_ready, TH)
            rows(0, 0, True)
            pe.wait_ge(v_split, 1)
            project_v(0, 1)
            for j in range(2):
                scores_t(0, 0, j)

            def unit(b, h, more):
                n = PER * b + JT * h
                nh = 1 - h
                nb = b + h
                has_scores = more or h == 0
                for j in range(JT):
                    if j < TH and has_scores:
                        T = JT * nb + TH * nh + j
                        if j == 0 and h == 0:
                            pe.wait_ge(row_put, 2 * b + 1)
                        elif j == 1 and h == 0:
                            pe.wait_ge(v_split, 2 * b + 2)
                        elif j == 0:
                            for half in range(2):
                                pe.wait_ge(a_in[half], 6 * DMA * (b + 2))
                            pe.wait_ge(qk_split, 2 * b + 4)
                        elif j == 1:
                            pe.wait_ge(row_put, 2 * b + 2)
                        else:
                            pe.wait_ge(rowsum_ready, T - 1)
                        scores(T, TH * nh + j)
                    if h == 0 and more and j in (TH, TH + 1):
                        project_qk(b + 1, j - TH, False)
                    if h == 1 and more and j == TH:
                        pe.wait_ge(rowsum_ready, JT * (b + 1) + TH - 1)
                        project_v(b + 1, 0)
                    if j == 0:
                        pe.wait_ge(acc_read, 2 * (2 * b + h))
                    weigh_v(b, h, j)
                    if j == JT - 2 and has_scores:
                        if h == 0 and more:
                            pe.wait_ge(qk_split, 2 * b + 3)
                        else:
                            pe.wait_ge(rowsum_ready, JT * nb + TH * nh + (TH if h else TH - 1))
                        rows(nb, nh, False)
                    if h == 1 and more and j == JT - 1:
                        pe.wait_ge(v_split, 2 * b + 3)
                        project_v(b + 1, 1)
                    ahead = j + 2
                    if ahead < JT or has_scores:
                        pe.wait_ge(exp_done, n + j + 1)
                        if ahead < JT:
                            scores_t(b, h, ahead)
                        else:
                            scores_t(nb, nh, ahead - JT)

            with pe.Fori(0, BATCH - 1) as b:
                unit(b, 0, True)
                unit(b, 1, True)
            unit(BATCH - 1, 0, False)
            unit(BATCH - 1, 1, False)


_OUT = (4, 256, 32, 32)


def kernel(x, L0_conv_Wq, L0_conv_bq, L0_conv_Wk, L0_conv_bk, L0_conv_Wv, L0_conv_bv):
    import numpy as np
    import concourse.bacc as bacc
    from concourse.bass_utils import run_bass_kernel_spmd

    x, wq, bq, wk, bk, wv, bv = (np.asarray(a) for a in (
        x, L0_conv_Wq, L0_conv_bq, L0_conv_Wk, L0_conv_bk, L0_conv_Wv, L0_conv_bv))
    images, channels = x.shape[:2]
    arrays = {
        "x": np.ascontiguousarray(x.reshape(images, channels, -1)),
        "wqk_t": np.ascontiguousarray(np.concatenate([wq, wk, wq, wk], axis=0).T),
        "bias_qk": np.ascontiguousarray(np.concatenate([bq, bk, bq, bk])[:, None]),
        "wv_t": np.ascontiguousarray(wv.T),
        "bv": np.ascontiguousarray(bv.reshape(-1, 128).T),
    }
    nc = bacc.Bacc("TRN2", target_bir_lowering=False, num_devices=1)
    args = [nc.dram_tensor(n, a.shape, mybir.dt.from_np(a.dtype), kind="ExternalInput").ap() for n, a in arrays.items()]
    out = nc.dram_tensor("out", arrays["x"].shape, mybir.dt.float32, kind="ExternalOutput").ap()
    nonlocal_attention(nc, *args, out)
    r = run_bass_kernel_spmd(nc, [arrays], core_ids=[0])
    return r.results[0]["out"].reshape(x.shape)
```

```python
from contextlib import ExitStack

import concourse.bass as bass
from concourse import mybir


def nonlocal_attention(nc, x, wqk_t, bias_qk, wv_t, bv, out):
    fp32 = mybir.dt.float32
    fp32r = mybir.dt.float32r
    ALU = mybir.AluOpType
    ACT = mybir.ActivationFunctionType
    AX = mybir.AxisListType

    P = 128
    BATCH, C, N = x.shape
    CQK = C // 8
    CT = C // P
    HALF = N // 2
    JT = N // P
    TH = JT // 2
    PER = 2 * JT
    IDLE_PRODUCTS = 9
    FILL = (3, 4)
    RING = 4
    AHEAD = 2
    SHIFT = 3 * CQK
    K_A = SHIFT
    K_B = SHIFT + 2
    DMA = 16
    HI, LO = 0, 1
    QUARTER = N // 4

    PARTS, Q_STACK, K_STACK = 0, 1, 2
    WEIGHTS = {PARTS: slice(CQK, 5 * CQK), Q_STACK: slice(0, 3 * CQK), K_STACK: slice(3 * CQK, 6 * CQK)}
    LOW = {PARTS: (1, 3), Q_STACK: (1,), K_STACK: (2,)}

    CUT_BY_ACT = (0, 1, 9, 11)
    SPLIT_BY_POOL = (0, 1, 10, 12)

    S, QK, V, ROW = "scores", "project q, k", "project v", "shifts to rows"
    FRONT = {0: (S, 6, 0), 1: (S, 7, 0), 2: (QK, 0, 1), 3: (QK, 1, 1),
             7: (S, 0, 1), 8: (S, 1, 1), 9: (S, 2, 1), 10: (S, 3, 1), 11: (V, 0, 1),
             12: (S, 4, 1), 14: (S, 5, 1), 15: (V, 1, 1)}
    SLOT = {item[:2]: n % 2 for n, item in enumerate(FRONT.values())}
    ROWS = {5: (ROW, 1, 0), 13: (ROW, 0, 1)}

    x_v = x.rearrange("b (t p) n -> b p t n", p=P)
    out_v = out.rearrange("b (t p) n -> b p t n", p=P)

    ctx = ExitStack()
    with ctx:
        def sb(name, shape, dt=fp32):
            return ctx.enter_context(nc.sbuf_tensor(name, shape, dt))

        def sem(name):
            return ctx.enter_context(nc.semaphore(name))

        x_sb = sb("x_sb", [P, BATCH, CT, N])
        x_hi = sb("x_hi", [P, CT, N], fp32r)
        x_lo = sb("x_lo", [P, CT, N], fp32r)
        wqk = sb("wqk", [P, CT, 6 * CQK])
        wqk_hi = sb("wqk_hi", [P, CT, 6 * CQK], fp32r)
        wqk_lo = sb("wqk_lo", [P, CT, 6 * CQK], fp32r)
        wv = sb("wv", [P, CT, C])
        wv_hi = sb("wv_hi", [P, CT, C], fp32r)
        wv_lo = sb("wv_lo", [P, CT, C], fp32r)
        bias = sb("bias", [P, 3])
        lo_rows = sb("lo_rows", [P, 3])
        lo_bias = sb("lo_bias", [P, 3])
        idle = sb("idle", [P, HALF], mybir.dt.bfloat16)
        bv_sb = sb("bv_sb", [P, CT])
        eye = sb("eye", [P, P])
        eye_r = sb("eye_r", [P, P], fp32r)
        ones = sb("ones", [P, N])
        qk_cut = sb("qk_cut", [P, N], fp32r)
        q_cut = sb("q_cut", [P, N], fp32r)
        qk_parts = sb("qk_parts", [P, N], fp32r)
        q_a = sb("q_a", [P, N], fp32r)
        k_a = sb("k_a", [P, N], fp32r)
        q_b = sb("q_b", [P, N], fp32r)
        k_b = sb("k_b", [P, N], fp32r)
        v_hi = sb("v_hi", [P, JT, C], fp32r)
        v_lo = sb("v_lo", [P, JT, C], fp32r)
        dump = sb("dump", [P, 2, N])
        negmax = sb("negmax", [P, JT])
        rowsum = sb("rowsum", [P, JT])
        logsum = sb("logsum", [P, JT])
        shift = sb("shift", [P, JT])
        shift_parts = sb("shift_parts", [P, JT, 2], fp32r)
        w_full = sb("w_full", [P, RING, HALF])
        w_hi = sb("w_hi", [P, RING, HALF], fp32r)
        w_lo = sb("w_lo", [P, RING, HALF], fp32r)
        o_sb = sb("o_sb", [P, 2, CT, HALF])

        acc = ctx.enter_context(nc.psum_tensor("acc", [P, CT, HALF], fp32))
        st = ctx.enter_context(nc.psum_tensor("st", [P, 2, HALF], fp32))
        slot = [ctx.enter_context(nc.psum_tensor(f"slot{i}", [P, N], fp32)) for i in range(2)]

        x0_in = [sem(f"x0_in{i}") for i in range(4)]
        x_in = sem("x_in")
        wqk_in = sem("wqk_in")
        wv_in = sem("wv_in")
        bias_in = sem("bias_in")
        bv_in = sem("bv_in")
        consts = sem("consts")
        eye_made = sem("eye_made")
        ones_put = sem("ones_put")
        wcut = sem("wcut")
        wsplit = sem("wsplit")
        x_cut = sem("x_cut")
        x0_split = sem("x0_split")
        x_split = sem("x_split")
        stack_ready = sem("stack_ready")
        stack_cut = sem("stack_cut")
        stack_split = sem("stack_split")
        v_part_ready = sem("v_part_ready")
        v_part_cut = sem("v_part_cut")
        qk_ready = sem("qk_ready")
        qk_cut_done = sem("qk_cut_done")
        qk_split = sem("qk_split")
        qa_in = [sem("qa_in0"), sem("qa_in1")]
        ka_in = [sem("ka_in0"), sem("ka_in1")]
        qb_in = [sem("qb_in0"), sem("qb_in1")]
        kb_in = [sem("kb_in0"), sem("kb_in1")]
        scores_ready = sem("scores_ready")
        negmax_ready = sem("negmax_ready")
        rowsum_ready = sem("rowsum_ready")
        logsum_ready = sem("logsum_ready")
        shift_full = sem("shift_full")
        shift_cut = sem("shift_cut")
        shift_ready = sem("shift_ready")
        row_ready = sem("row_ready")
        row_put = sem("row_put")
        v_ready = sem("v_ready")
        v_cut = sem("v_cut")
        v_split = sem("v_split")
        st_ready = sem("st_ready")
        exp_done = sem("exp_done")
        w_cut_act = sem("w_cut_act")
        w_cut_dve = sem("w_cut_dve")
        w_split_dve = sem("w_split_dve")
        w_split_pool = sem("w_split_pool")
        av_done = sem("av_done")
        acc0_ready = sem("acc0_ready")
        acc_read = sem("acc_read")
        out_sent = [sem("out_sent0"), sem("out_sent1")]
        sp_passed = sem("sp_passed")
        pool_passed = sem("pool_passed")
        act_passed = sem("act_passed")

        PRE = RING

        def cols(h):
            return slice(h * HALF, (h + 1) * HALF)

        def front(s, more):
            what, k, image = (FRONT | ROWS).get(s, (None, 0, 0))
            return (what, k, image) if image == 0 or more else (None, 0, 0)

        def place(s, b):
            return b + s // PER, s % PER // JT, s % JT

        def quarter(i):
            return slice(i * QUARTER, (i + 1) * QUARTER)

        def flat(banks):
            return banks[:, :, :].rearrange("p i n -> p (i n)")

        FIRST_HOME = {0: flat(acc), 1: slot[1][:, :], 2: flat(st), 3: flat(acc), 4: slot[0][:, :], 5: slot[1][:, :]}
        STACKS = [(K_STACK, 0), (Q_STACK, 0), (K_STACK, 1), (Q_STACK, 1)]
        STACK_SLOT = {K_STACK: slot[1], Q_STACK: slot[0]}
        STACK_CUT = {K_STACK: qk_cut, Q_STACK: q_cut}
        STACK_DST = {K_STACK: k_a, Q_STACK: q_a}

        def s_home(t, first):
            return FIRST_HOME[t] if first else slot[SLOT[S, t]][:, :]

        def v_home(g):
            return slot[SLOT[V, g]][:, :]

        def made(mine, b, tile):
            return len(mine) * (b + tile // PER) + sum(j <= tile % PER for j in mine)

        def last_ring(mine):
            return sum(j >= PER - RING for j in mine)

        CUT_BY_DVE = [j for j in range(PER) if j not in CUT_BY_ACT]
        SPLIT_BY_DVE = [j for j in range(PER) if j not in SPLIT_BY_POOL]

        def wait_w_cut(engine, b, tile):
            if tile % PER in CUT_BY_ACT:
                engine.wait_ge(w_cut_act, made(CUT_BY_ACT, b, tile))
            else:
                engine.wait_ge(w_cut_dve, made(CUT_BY_DVE, b, tile))

        def wait_w_split(engine, b, tile):
            if tile % PER in SPLIT_BY_POOL:
                engine.wait_ge(w_split_pool, last_ring(SPLIT_BY_POOL) + made(SPLIT_BY_POOL, b, tile))
            else:
                engine.wait_ge(w_split_dve, last_ring(SPLIT_BY_DVE) + made(SPLIT_BY_DVE, b, tile))

        block = ctx.enter_context(nc.Block())

        @block.sync
        def _(sp):
            for h in range(2):
                sp.sem_inc(out_sent[h], 1)
            sp.dma_start(wqk[:, :, :], wqk_t.rearrange("(t p) m -> p t m", p=P)).then_inc(wqk_in, DMA)
            for i in range(4):
                sp.dma_start(x_sb[:, 0, :, quarter(i)], x_v[0, :, :, quarter(i)]).then_inc(x0_in[i], DMA)
            sp.dma_start(wv[:, :, :], wv_t.rearrange("(t p) m -> p t m", p=P)).then_inc(wv_in, DMA)

            def stack(dst, row, src_row, n, h, done):
                sp.dma_start(dst[row * CQK:(row + n) * CQK, cols(h)].bitcast(fp32),
                             qk_parts[src_row * CQK:(src_row + n) * CQK, cols(h)].bitcast(fp32)).then_inc(done, DMA)

            def q_stack(dst, h, done):
                stack(dst, 0, 0, 2, h, done)
                stack(dst, 2, 0, 1, h, done)

            def k_stack(dst, h, done):
                stack(dst, 0, 2, 1, h, done)
                stack(dst, 1, 2, 2, h, done)

            def wait(done, count):
                sp.wait_ge(done, count)
                sp.sem_inc(sp_passed, 1)

            def stacks_a(b):
                for h in range(2):
                    wait(qk_split, 2 * b + h - 1)
                    if h == 0:
                        wait(scores_ready, JT * b)
                    k_stack(k_a, h, ka_in[h])
                    q_stack(q_a, h, qa_in[h])

            for n, (kind, h) in enumerate(STACKS):
                dst, done = (k_b, kb_in) if kind == K_STACK else (q_b, qb_in)
                sp.wait_ge(stack_split, n + 1)
                sp.dma_start(dst[0:SHIFT, cols(h)].bitcast(fp32),
                             STACK_DST[kind][0:SHIFT, cols(h)].bitcast(fp32)).then_inc(done[h], DMA)

            for b in range(1, BATCH):
                sp.dma_start(x_sb[:, b, :, :], x_v[b]).then_inc(x_in, DMA)
                sp.wait_ge(x_in, DMA * b)

            def send(b, h):
                wait(acc_read, 2 * (2 * b + h) + 4)
                sp.dma_start(out_v[b, :, :, cols(h)], o_sb[:, h, :, :]).then_inc(out_sent[h], DMA)

            with sp.Fori(0, BATCH - 1) as b:
                stacks_a(b + 1)
                wait(st_ready, PER * b + JT)
                q_stack(q_b, 0, qb_in[0])
                send(b, 0)
                wait(st_ready, PER * b + JT + TH)
                k_stack(k_b, 0, kb_in[0])
                wait(st_ready, PER * b + PER)
                k_stack(k_b, 1, kb_in[1])
                q_stack(q_b, 1, qb_in[1])
                send(b, 1)
            send(BATCH - 1, 0)
            send(BATCH - 1, 1)
            for h in range(2):
                sp.wait_ge(out_sent[h], DMA * BATCH + 1)

        @block.gpsimd
        def _(pool):
            if last_ring(SPLIT_BY_POOL):
                pool.sem_inc(w_split_pool, last_ring(SPLIT_BY_POOL))
            pool.dma_start(bias[:, :], bias_qk).then_inc(bias_in, DMA)
            nc.gpsimd.memset(eye[:, :], 0.0).then_inc(eye_made, 1)
            pool.wait_ge(eye_made, 1)
            nc.gpsimd.affine_select(out=eye[:, :], in_=eye[:, :], compare_op=ALU.not_equal, fill=1.0,
                                    base=0, pattern=[[-1, P]], channel_multiplier=1).then_inc(eye_made, 1)
            for h in range(2):
                pool.wait_ge(x_cut, h + 3)
                nc.gpsimd.tensor_tensor(x_lo[:, :, quarter(h + 2)], x_sb[:, 0, :, quarter(h + 2)],
                                        x_hi[:, :, quarter(h + 2)].bitcast(fp32), ALU.subtract).then_inc(x_split, 1)
            pool.dma_start(bv_sb[:, :], bv).then_inc(bv_in, DMA)
            def split_w(b, tile):
                if tile % PER not in SPLIT_BY_POOL:
                    return
                n, j = PER * b + tile, tile % JT
                pool.wait_ge(exp_done, n + 1)
                wait_w_cut(pool, b, tile)
                pool.wait_ge(av_done, n + 1)
                nc.gpsimd.tensor_tensor(w_lo[:, j % RING, :], w_full[:, j % RING, :],
                                        w_hi[:, j % RING, :].bitcast(fp32), ALU.subtract).then_inc(w_split_pool, 1)

            for j in range(AHEAD):
                split_w(0, j)

            with pool.Fori(0, BATCH - 1) as b:
                for h in range(2):
                    pool.wait_ge(x_cut, 2 * b + h + 5)
                    pool.sem_inc(pool_passed, 1)
                    nc.gpsimd.tensor_tensor(x_lo[:, :, cols(h)], x_sb[:, b + 1, :, cols(h)],
                                            x_hi[:, :, cols(h)].bitcast(fp32), ALU.subtract).then_inc(x_split, 1)
                for s in range(PER):
                    split_w(b, s + AHEAD)
            for s in range(PER - AHEAD):
                split_w(BATCH - 1, s + AHEAD)

        @block.scalar
        def _(act):
            act.preload_act_table_set("natural_log_exp_and_others")
            act.wait_ge(consts, 2)
            nc.scalar.activation(k_b[SHIFT:K_B, :], ones[SHIFT:K_B, :], ACT.Copy).then_inc(ones_put, 1)
            act.wait_ge(wqk_in, DMA)
            nc.scalar.activation(wqk_hi[:, :, :], wqk[:, :, :], ACT.Copy).then_inc(wcut, 1)
            for i in range(4):
                act.wait_ge(x0_in[i], DMA)
                nc.scalar.activation(x_hi[:, :, quarter(i)], x_sb[:, 0, :, quarter(i)], ACT.Copy).then_inc(x_cut, 1)

            def cut_stack(n):
                kind, h = STACKS[n]
                act.wait_ge(stack_ready, n + 1)
                if n == 0:
                    act.wait_ge(wsplit, 2)
                nc.scalar.activation(STACK_CUT[kind][0:SHIFT, cols(h)], STACK_SLOT[kind][0:SHIFT, cols(h)], ACT.Identity,
                                     bias=lo_bias[0:SHIFT, kind:kind + 1],
                                     scale=lo_rows[0:SHIFT, kind:kind + 1]).then_inc(stack_cut, 1)

            def cut_qk(b, h):
                act.wait_ge(qk_ready, 2 * b + h - 1)
                nc.scalar.activation(qk_cut[:, cols(h)], slot[SLOT[QK, h]][:, 0:HALF], ACT.Identity,
                                     bias=lo_bias[:, 0:1], scale=lo_rows[:, 0:1]).then_inc(qk_cut_done, 1)

            def sum_exp(b, t, first=False):
                act.wait_ge(negmax_ready, JT * b + t + 1)
                if first and t in (2, 3):
                    act.wait_ge(rowsum_ready, t - 1)
                nc.scalar.activation(dump[:, t % 2, :], s_home(t, first), ACT.Exp,
                                     bias=negmax[:, t:t + 1], accum_out=rowsum[:, t:t + 1]).then_inc(rowsum_ready, 1)

            def log_sums(b, h):
                act.wait_ge(rowsum_ready, JT * b + TH * h + TH)
                nc.scalar.activation(logsum[:, TH * h:TH * h + TH], rowsum[:, TH * h:TH * h + TH],
                                     ACT.Ln).then_inc(logsum_ready, 1)

            def put_rows(b, h):
                act.wait_ge(row_ready, 2 * b + h + 1)
                nc.scalar.activation(q_b[SHIFT:K_B, cols(h)], st[0:2, 0, :], ACT.Copy).then_inc(row_put, 1)

            def cut_v(b, g, first=False, tiles=(0, TH)):
                if tiles[1] < TH:
                    act.wait_ge(v_part_ready, g + 1)
                else:
                    act.wait_ge(v_ready, 2 * b + g + 1)
                if not first:
                    act.wait_ge(av_done, PRE + PER * (b - 1) + JT + TH * g + TH)
                nc.scalar.activation(v_hi[:, TH * g + tiles[0]:TH * g + tiles[1], :],
                                     v_home(g)[:, tiles[0] * C:tiles[1] * C].rearrange("p (j c) -> p j c", c=C),
                                     ACT.Copy).then_inc(v_part_cut if tiles[1] < TH else v_cut, 1)

            def exp(b, tile):
                n, j = PER * b + tile, tile % JT
                act.wait_ge(st_ready, n + 1)
                if tile % PER in CUT_BY_ACT:
                    act.wait_ge(av_done, n + 1)
                    nc.scalar.activation(w_hi[:, j % RING, :], st[:, j % 2, :], ACT.Exp).then_inc(w_cut_act, 1)
                wait_w_split(act, b, tile - RING)
                nc.scalar.activation(w_full[:, j % RING, :], st[:, j % 2, :], ACT.Exp).then_inc(exp_done, 1)

            def cut_x(b, h):
                if h == 0:
                    act.wait_ge(x_in, DMA * b)
                    act.wait_ge(v_ready, 2 * b)
                    act.sem_inc(act_passed, 1)
                nc.scalar.activation(x_hi[:, :, cols(h)], x_sb[:, b, :, cols(h)], ACT.Copy).then_inc(x_cut, 1)

            cut_stack(0)
            act.wait_ge(wv_in, DMA)
            nc.scalar.activation(wv_hi[:, :, :], wv[:, :, :], ACT.Copy).then_inc(wcut, 1)
            for n in range(1, 4):
                cut_stack(n)
            act.wait_ge(eye_made, 2)
            nc.scalar.activation(eye_r[:, :], eye[:, :], ACT.Copy).then_inc(wcut, 1)
            sum_exp(0, 0, True)
            sum_exp(0, 1, True)
            cut_v(0, 0, True, (0, 2))
            sum_exp(0, 2, True)
            sum_exp(0, 3, True)
            log_sums(0, 0)
            cut_v(0, 0, True, (2, TH))
            cut_v(0, 1, True, (0, 2))
            put_rows(0, 0)
            cut_v(0, 1, True, (2, TH))
            for j in range(AHEAD):
                exp(0, j)
            for j in range(2):
                sum_exp(0, TH + j, True)

            def turn(b, more):
                for s in range(PER):
                    if s + AHEAD < PER or more:
                        exp(b, s + AHEAD)
                    if more and s < 2:
                        cut_x(b + 1, s)
                    what, k, image = front(s, more)
                    if what == ROW:
                        put_rows(b + image, k)
                    what, t, image = front(s - 1, more)
                    if what == S:
                        sum_exp(b + image, t)
                        if t % TH == TH - 1:
                            log_sums(b + image, t // TH)
                    what, k, image = front(s, more)
                    if what == QK:
                        cut_qk(b + 1, k)
                    if what == V:
                        cut_v(b + 1, k)

            with act.Fori(0, BATCH - 1) as b:
                turn(b, True)
            turn(BATCH - 1, False)

        @block.vector
        def _(dve):
            dve.sem_inc(w_split_dve, last_ring(SPLIT_BY_DVE))
            nc.vector.memset(idle[:, :], 0.0).then_inc(consts, 1)
            nc.vector.memset(ones[SHIFT:SHIFT + 32, :], 1.0).then_inc(consts, 1)
            for kind, low in LOW.items():
                for row in range(4):
                    nc.vector.memset(lo_rows[row * CQK:(row + 1) * CQK, kind:kind + 1],
                                     float(row in low)).then_inc(consts, 1)
            dve.wait_ge(wcut, 1)
            nc.vector.tensor_tensor(wqk_lo[:, :, :], wqk[:, :, :], wqk_hi[:, :, :].bitcast(fp32),
                                    ALU.subtract).then_inc(wsplit, 1)
            dve.wait_ge(bias_in, DMA)
            dve.wait_ge(consts, 14)
            nc.vector.tensor_tensor(lo_bias[:, :], bias[:, :], lo_rows[:, :], ALU.mult).then_inc(wsplit, 1)
            for i in range(2):
                dve.wait_ge(x_cut, i + 1)
                nc.vector.tensor_tensor(x_lo[:, :, quarter(i)], x_sb[:, 0, :, quarter(i)],
                                        x_hi[:, :, quarter(i)].bitcast(fp32), ALU.subtract).then_inc(x0_split, 1)

            def split_stack(n):
                kind, h = STACKS[n]
                dve.wait_ge(stack_cut, n + 1)
                nc.vector.scalar_tensor_tensor(out=STACK_DST[kind][0:SHIFT, cols(h)],
                                               in0=STACK_SLOT[kind][0:SHIFT, cols(h)],
                                               scalar=bias[0:SHIFT, kind:kind + 1],
                                               in1=STACK_CUT[kind][0:SHIFT, cols(h)].bitcast(fp32),
                                               op0=ALU.add, op1=ALU.subtract).then_inc(stack_split, 1)

            def split_qk(b, h):
                dve.wait_ge(qk_cut_done, 2 * b + h - 1)
                dve.wait_ge(qb_in[h], DMA * (2 * b - 1))
                dve.wait_ge(kb_in[h], DMA * (2 * b - 1))
                nc.vector.scalar_tensor_tensor(out=qk_parts[:, cols(h)], in0=slot[SLOT[QK, h]][:, 0:HALF],
                                               scalar=bias[:, 0:1], in1=qk_cut[:, cols(h)].bitcast(fp32),
                                               op0=ALU.add, op1=ALU.subtract).then_inc(qk_split, 1)

            def row_max(b, t, first=False):
                dve.wait_ge(scores_ready, JT * b + t + 1)
                nc.vector.tensor_reduce(out=negmax[:, t:t + 1], in_=s_home(t, first),
                                        op=ALU.max, axis=AX.X, negate=True).then_inc(negmax_ready, 1)

            def shifts(b, h):
                part = slice(TH * h, TH * h + TH)
                dve.wait_ge(logsum_ready, 2 * b + h + 1)
                nc.vector.tensor_tensor(shift[:, part], negmax[:, part], logsum[:, part],
                                        ALU.subtract).then_inc(shift_full, 1)
                dve.wait_ge(shift_full, 2 * b + h + 1)
                nc.vector.tensor_copy(shift_parts[:, part, HI], shift[:, part]).then_inc(shift_cut, 1)
                dve.wait_ge(shift_cut, 2 * b + h + 1)
                nc.vector.tensor_tensor(shift_parts[:, part, LO], shift[:, part],
                                        shift_parts[:, part, HI].bitcast(fp32), ALU.subtract).then_inc(shift_ready, 1)

            def split_v(b, g, tiles=(0, TH)):
                if tiles[1] < TH:
                    dve.wait_ge(v_part_cut, g + 1)
                else:
                    dve.wait_ge(v_cut, 2 * b + g + 1)
                part = slice(TH * g + tiles[0], TH * g + tiles[1])
                split = nc.vector.tensor_tensor(
                    v_lo[:, part, :], v_home(g)[:, tiles[0] * C:tiles[1] * C].rearrange("p (j c) -> p j c", c=C),
                    v_hi[:, part, :].bitcast(fp32), ALU.subtract)
                if tiles[1] == TH:
                    split.then_inc(v_split, 1)

            def cut_w(b, tile):
                if tile % PER in CUT_BY_ACT:
                    return
                n, j = PER * b + tile, tile % JT
                dve.wait_ge(exp_done, n + 1)
                dve.wait_ge(av_done, n + 1)
                nc.vector.tensor_copy(w_hi[:, j % RING, :], w_full[:, j % RING, :]).then_inc(w_cut_dve, 1)

            def split_w(b, tile):
                if tile % PER in SPLIT_BY_POOL:
                    return
                n, j = PER * b + tile, tile % JT
                dve.wait_ge(exp_done, n + 1)
                wait_w_cut(dve, b, tile)
                dve.wait_ge(av_done, n + 1)
                nc.vector.tensor_tensor(w_lo[:, j % RING, :], w_full[:, j % RING, :],
                                        w_hi[:, j % RING, :].bitcast(fp32), ALU.subtract).then_inc(w_split_dve, 1)

            def finish(b, h, c):
                if c == 0:
                    dve.wait_ge(acc0_ready, 2 * b + h + 1)
                else:
                    dve.wait_ge(av_done, PRE + PER * b + JT * h + JT)
                if c == 0:
                    dve.wait_ge(out_sent[h], DMA * b + 1)
                nc.vector.scalar_tensor_tensor(out=o_sb[:, h, c, :], in0=acc[:, c, :], scalar=bv_sb[:, c:c + 1],
                                               in1=x_sb[:, b, c, cols(h)], op0=ALU.add, op1=ALU.add).then_inc(acc_read, 1)

            split_stack(0)
            dve.wait_ge(wcut, 2)
            nc.vector.tensor_tensor(wv_lo[:, :, :], wv[:, :, :], wv_hi[:, :, :].bitcast(fp32),
                                    ALU.subtract).then_inc(wsplit, 1)
            split_stack(1)
            split_stack(2)
            row_max(0, 0, True)
            row_max(0, 1, True)
            split_stack(3)
            row_max(0, 2, True)
            row_max(0, 3, True)
            split_v(0, 0, (0, 2))
            shifts(0, 0)
            split_v(0, 0, (2, TH))
            split_v(0, 1, (0, 2))
            split_v(0, 1, (2, TH))
            dve.wait_ge(bv_in, DMA)
            for j in range(AHEAD):
                cut_w(0, j)
                row_max(0, TH + j, True)
                split_w(0, j)

            def turn(b, more):
                for s in range(PER):
                    what, k, image = front(s - 1, more)
                    before, t, its = front(s - 2, more)
                    summed = before == S and t % TH == TH - 1
                    if summed:
                        shifts(b + its, t // TH)
                    ahead = s + AHEAD < PER or more
                    if s % JT == JT - 1:
                        for c in range(CT):
                            finish(b, s // JT, c)
                    if ahead:
                        cut_w(b, s + AHEAD)
                    if what == QK:
                        split_qk(b + 1, k)
                    if ahead:
                        split_w(b, s + AHEAD)
                    if what == V:
                        split_v(b + 1, k)
                    what, k, image = front(s, more)
                    if what == S:
                        row_max(b + image, k)
                    if s == PER - 1 and more:
                        split_v(b + 1, 1)

            with dve.Fori(0, BATCH - 1) as b:
                turn(b, True)
            turn(BATCH - 1, False)

        @block.tensor
        def _(pe):
            pe.sem_inc(av_done, PRE)
            pe.sem_inc(acc_read, 2)

            def group(dst, terms):
                for i, (lhs, rhs) in enumerate(terms):
                    last = nc.tensor.matmul(dst, lhs, rhs, start=(i == 0), stop=(i == len(terms) - 1))
                return last

            def project_stack(n):
                kind, h = STACKS[n]
                w, x = WEIGHTS[kind], cols(h)
                dst = STACK_SLOT[kind][0:SHIFT, x]
                if n == 0:
                    pe.wait_ge(wcut, 1)
                if n in (0, 2):
                    pe.wait_ge(x_cut, n + 2)
                for c in range(CT):
                    nc.tensor.matmul(dst, wqk_hi[:, c, w], x_hi[:, c, x], start=(c == 0), stop=False)
                if n == 0:
                    pe.wait_ge(wsplit, 1)
                for c in range(CT):
                    nc.tensor.matmul(dst, wqk_lo[:, c, w], x_hi[:, c, x], start=False, stop=False)
                if n in (0, 2):
                    pe.wait_ge(x0_split if h == 0 else x_split, 2)
                for c in range(CT):
                    last = nc.tensor.matmul(dst, wqk_hi[:, c, w], x_lo[:, c, x], start=False, stop=(c == CT - 1))
                last.then_inc(stack_ready, 1)

            def project_qk(b, h):
                pe.wait_ge(x_split, 2 * b + h + 1)
                pe.wait_ge(rowsum_ready, JT * b - 1 + h)
                m = WEIGHTS[PARTS]
                terms = [(w[:, c, m], xs[:, c, cols(h)]) for c in range(CT)
                         for w, xs in ((wqk_hi, x_hi), (wqk_lo, x_hi), (wqk_hi, x_lo))]
                group(slot[SLOT[QK, h]][:, 0:HALF], terms).then_inc(qk_ready, 1)

            def scores(b, t):
                if t == 0:
                    pe.wait_ge(qa_in[0], 2 * DMA * b)
                    pe.wait_ge(ka_in[0], 2 * DMA * b)
                    pe.wait_ge(ka_in[1], 2 * DMA * b)
                elif t in (2, 3):
                    pe.wait_ge(rowsum_ready, JT * b + t - 1)
                elif t in (4, 6):
                    pe.wait_ge(rowsum_ready, JT * b + t)
                if t == TH:
                    pe.wait_ge(qa_in[1], 2 * DMA * b)
                if t in (5, 7):
                    pe.wait_ge(v_split, 2 * b + (t - 3) // 2)
                for h in range(2):
                    last = nc.tensor.matmul(s_home(t, False)[:, cols(h)], q_a[0:K_A, t * P:(t + 1) * P],
                                            k_a[0:K_A, cols(h)], start=True, stop=True)
                last.then_inc(scores_ready, 1)

            def first_scores(t):
                for h in range(2):
                    if t == 0:
                        pe.wait_ge(stack_split, h + 2)
                    if t == 3 and h == 0:
                        pe.wait_ge(rowsum_ready, 1)
                    if t in (4, 5) and h == 0:
                        pe.wait_ge(v_split, t - 3)
                    last = nc.tensor.matmul(s_home(t, True)[:, cols(h)], q_a[0:K_A, t * P:(t + 1) * P],
                                            k_a[0:K_A, cols(h)], start=True, stop=True)
                last.then_inc(scores_ready, 1)

            def v_tile(g, jj):
                px = slice((TH * g + jj) * P, (TH * g + jj + 1) * P)
                terms = [(xs[:, c, px], w[:, c, :]) for c in range(CT)
                         for xs, w in ((x_hi, wv_hi), (x_hi, wv_lo), (x_lo, wv_hi))]
                return group(v_home(g)[:, jj * C:(jj + 1) * C], terms)

            def project_v(b, g):
                pe.wait_ge(rowsum_ready, JT * b + 3 + 2 * g)
                for jj in range(TH):
                    last = v_tile(g, jj)
                last.then_inc(v_ready, 1)

            def rows(b, h, first=False):
                pe.wait_ge(shift_ready, 2 * b + h + 1)
                if first:
                    pe.wait_ge(wcut, 3)
                    pe.wait_ge(ones_put, 1)
                    pe.wait_ge(rowsum_ready, 3)
                else:
                    pe.wait_ge(exp_done, PER * b + JT * h - 1)
                for t in range(TH):
                    last = nc.tensor.matmul(st[0:2, 0, t * P:(t + 1) * P], shift_parts[:, TH * h + t, :],
                                            eye_r[:, :], start=True, stop=True)
                last.then_inc(row_ready, 1)

            def scores_t(b, h, j):
                if j == 0:
                    pe.wait_ge(row_put, 2 * b + h + 1)
                    pe.wait_ge(qb_in[h], DMA * (2 * b + 1))
                    if h == 0:
                        pe.wait_ge(kb_in[0], DMA * (2 * b + 1))
                if j == TH and h == 0:
                    pe.wait_ge(kb_in[1], DMA * (2 * b + 1))
                nc.tensor.matmul(st[:, j % 2, :], k_b[0:K_B, j * P:(j + 1) * P], q_b[0:K_B, cols(h)],
                                 start=True, stop=True).then_inc(st_ready, 1)

            def weigh_v(b, h, j):
                n = PER * b + JT * h + j
                r = j % RING
                if h == 0 and j in (0, TH):
                    pe.wait_ge(v_split, 2 * b + 1 + j // TH)
                wait_w_cut(pe, b, JT * h + j)
                for c in range(CT):
                    ch = slice(c * P, (c + 1) * P)
                    if j == 0:
                        pe.wait_ge(acc_read, 2 * (2 * b + h) + c + 1)
                    for v in (v_hi, v_lo):
                        nc.tensor.matmul(acc[:, c, :], v[:, j, ch], w_hi[:, r, :],
                                         start=(j == 0 and v is v_hi), stop=False)
                    if j == JT - 1 and c == 0:
                        wait_w_split(pe, b, JT * h + j)
                        nc.tensor.matmul(acc[:, c, :], v_hi[:, j, ch], w_lo[:, r, :],
                                         start=False, stop=True).then_inc(acc0_ready, 1)
                wait_w_split(pe, b, JT * h + j)
                for c in range(1 if j == JT - 1 else 0, CT):
                    last = nc.tensor.matmul(acc[:, c, :], v_hi[:, j, c * P:(c + 1) * P], w_lo[:, r, :],
                                            start=False, stop=(j == JT - 1))
                last.then_inc(av_done, 1)

            def keep_busy(count, bank):
                for i in range(count):
                    nc.tensor.matmul(bank, idle[:, 0:P], idle[:, :], start=True, stop=True)

            pe.wait_ge(consts, 1)
            keep_busy(IDLE_PRODUCTS, st[:, 0, :])
            for n in range(4):
                project_stack(n)
            for t in range(3):
                first_scores(t)
            pe.wait_ge(wsplit, 3)
            for jj in range(2):
                last = v_tile(0, jj)
            last.then_inc(v_part_ready, 1)
            first_scores(3)
            pe.wait_ge(stack_split, 4)
            for jj in range(2, TH):
                last = v_tile(0, jj)
            last.then_inc(v_ready, 1)
            pe.wait_ge(rowsum_ready, 2)
            for jj in range(TH):
                last = v_tile(1, jj)
                if jj == 1:
                    last.then_inc(v_part_ready, 1)
            last.then_inc(v_ready, 1)
            rows(0, 0, True)
            keep_busy(FILL[0], st[:, 1, :])
            for j in range(AHEAD):
                scores_t(0, 0, j)
            first_scores(TH)
            keep_busy(FILL[1], acc[:, 0, :])
            first_scores(TH + 1)

            def turn(b, more):
                for s in range(PER):
                    if s + AHEAD < PER or more:
                        pe.wait_ge(exp_done, PER * b + s + AHEAD - 1)
                        scores_t(*place(s + AHEAD, b))
                    what, k, image = front(s, more)
                    if what == ROW:
                        rows(b + image, k)
                    weigh_v(b, s // JT, s % JT)
                    if what == S:
                        scores(b + image, k)
                    elif what == QK:
                        project_qk(b + 1, k)
                    elif what == V:
                        project_v(b + 1, k)

            with pe.Fori(0, BATCH - 1) as b:
                turn(b, True)
            turn(BATCH - 1, False)


_OUT = (4, 256, 32, 32)


def kernel(x, L0_conv_Wq, L0_conv_bq, L0_conv_Wk, L0_conv_bk, L0_conv_Wv, L0_conv_bv):
    import numpy as np
    import concourse.bacc as bacc
    from concourse.bass_utils import run_bass_kernel_spmd

    x, wq, bq, wk, bk, wv, bv = (np.asarray(a) for a in (
        x, L0_conv_Wq, L0_conv_bq, L0_conv_Wk, L0_conv_bk, L0_conv_Wv, L0_conv_bv))
    images, channels = x.shape[:2]
    arrays = {
        "x": np.ascontiguousarray(x.reshape(images, channels, -1)),
        "wqk_t": np.ascontiguousarray(np.concatenate([wq] * 3 + [wk] * 3, axis=0).T),
        "bias_qk": np.ascontiguousarray(np.stack([np.concatenate([bq, bq, bk, bk]), np.concatenate([bq] * 4),
                                                   np.concatenate([bk] * 4)], axis=1)),
        "wv_t": np.ascontiguousarray(wv.T),
        "bv": np.ascontiguousarray(bv.reshape(-1, 128).T),
    }
    nc = bacc.Bacc("TRN2", target_bir_lowering=False, num_devices=1)
    args = [nc.dram_tensor(n, a.shape, mybir.dt.from_np(a.dtype), kind="ExternalInput").ap() for n, a in arrays.items()]
    out = nc.dram_tensor("out", arrays["x"].shape, mybir.dt.float32, kind="ExternalOutput").ap()
    nonlocal_attention(nc, *args, out)
    r = run_bass_kernel_spmd(nc, [arrays], core_ids=[0])
    return r.results[0]["out"].reshape(x.shape)
```

```python
from contextlib import ExitStack

import concourse.bass as bass
from concourse import mybir



def nonlocal_attention(nc, x, wqk_t, bias_qk, wv_t, bv, out):
    fp32 = mybir.dt.float32
    fp32r = mybir.dt.float32r
    ALU = mybir.AluOpType
    ACT = mybir.ActivationFunctionType
    AX = mybir.AxisListType

    P = 128
    BATCH, C, N = x.shape
    CQK = C // 8
    CT = C // P
    HALF = N // 2
    JT = N // P
    TH = JT // 2
    VT = HALF // C
    PER = 2 * JT
    RING = 8
    AHEAD = 2
    SHIFT = 3 * CQK
    K_A = SHIFT
    K_B = SHIFT + 2
    DMA = 16
    LOAD_PRODUCTS = 8
    WAIT_PRODUCTS = 8
    HI, LO = 0, 1
    QUARTER = N // 4

    LOW, FIRST_LOW = 0, 1
    LOW_BLOCKS = {LOW: (1, 3), FIRST_LOW: (1, 2, 3)}

    CUT_BY_ACT = (0, 9, 11)
    SPLIT_BY_POOL = (0, 9, 11, 13)

    S, QK, V, ROW = "scores", "project q, k", "project v", "shifts to rows"
    FRONT = {0: (S, 6, 0), 1: (S, 7, 0), 2: (QK, 0, 1), 3: (QK, 1, 1),
             7: (S, 0, 1), 8: (S, 1, 1), 9: (S, 2, 1), 10: (S, 3, 1), 11: (V, 0, 1),
             12: (S, 4, 1), 14: (S, 5, 1), 15: (V, 1, 1)}
    SLOT = {item[:2]: n % 2 for n, item in enumerate(FRONT.values())}
    ROWS = {5: (ROW, 1, 0), 13: (ROW, 0, 1)}

    x_v = x.rearrange("b (t p) n -> b p t n", p=P)
    out_v = out.rearrange("b (t p) n -> b p t n", p=P)

    ctx = ExitStack()
    with ctx:
        def sb(name, shape, dt=fp32):
            return ctx.enter_context(nc.sbuf_tensor(name, shape, dt))

        def sem(name):
            return ctx.enter_context(nc.semaphore(name))

        x_sb = sb("x_sb", [P, BATCH, CT, N])
        x_hi = sb("x_hi", [P, CT, N], fp32r)
        x_lo = sb("x_lo", [P, CT, N], fp32r)
        wqk = sb("wqk", [P, CT, P])
        wqk_hi = sb("wqk_hi", [P, CT, P], fp32r)
        wqk_lo = sb("wqk_lo", [P, CT, P], fp32r)
        wv = sb("wv", [P, CT, C])
        wv_hi = sb("wv_hi", [P, CT, C], fp32r)
        wv_lo = sb("wv_lo", [P, CT, C], fp32r)
        bias = sb("bias", [P, 1])
        lo_rows = sb("lo_rows", [P, 2])
        lo_bias = sb("lo_bias", [P, 2])
        idle = sb("idle", [P, HALF], mybir.dt.bfloat16)
        bv_sb = sb("bv_sb", [P, CT])
        eye = sb("eye", [P, P])
        eye_r = sb("eye_r", [P, P], fp32r)
        ones = sb("ones", [P, N])
        qk_cut = sb("qk_cut", [P, N], fp32r)
        qk_parts = sb("qk_parts", [P, N], fp32r)
        q_a = sb("q_a", [P, N], fp32r)
        k_a = sb("k_a", [P, N], fp32r)
        q_b = sb("q_b", [P, N], fp32r)
        k_b = sb("k_b", [P, N], fp32r)
        v_hi = sb("v_hi", [P, JT, C], fp32r)
        v_lo = sb("v_lo", [P, JT, C], fp32r)
        dump = sb("dump", [P, 2, N])
        negmax = sb("negmax", [P, JT])
        rowsum = sb("rowsum", [P, JT])
        logsum = sb("logsum", [P, JT])
        shift = sb("shift", [P, JT])
        shift_parts = sb("shift_parts", [P, JT, 2], fp32r)
        w_full = sb("w_full", [P, RING, HALF])
        w_hi = sb("w_hi", [P, RING, HALF], fp32r)
        w_lo = sb("w_lo", [P, RING, HALF], fp32r)
        o_sb = sb("o_sb", [P, 2, CT, HALF])

        acc = ctx.enter_context(nc.psum_tensor("acc", [P, CT, HALF], fp32))
        st = ctx.enter_context(nc.psum_tensor("st", [P, 2, HALF], fp32))
        slot = [ctx.enter_context(nc.psum_tensor(f"slot{i}", [P, N], fp32)) for i in range(2)]

        x0_in = [sem(f"x0_in{i}") for i in range(4)]
        x_in = sem("x_in")
        wqk_in = sem("wqk_in")
        wv_in = sem("wv_in")
        bias_in = sem("bias_in")
        bv_in = sem("bv_in")
        consts = sem("consts")
        eye_made = sem("eye_made")
        ones_put = sem("ones_put")
        wcut = sem("wcut")
        wsplit = sem("wsplit")
        wv_split = sem("wv_split")
        x_cut = sem("x_cut")
        x0_split = sem("x0_split")
        x_split = sem("x_split")
        q_put = sem("q_put")
        q_hi_put = [sem("q_hi_put0"), sem("q_hi_put1")]
        k_lo_put = sem("k_lo_put")
        k_hi_put = sem("k_hi_put")
        qk_ready = sem("qk_ready")
        qk_cut_done = sem("qk_cut_done")
        qk_split = sem("qk_split")
        qa_in = [sem("qa_in0"), sem("qa_in1")]
        ka_in = [sem("ka_in0"), sem("ka_in1")]
        qb_in = [sem("qb_in0"), sem("qb_in1")]
        kb_in = [sem("kb_in0"), sem("kb_in1")]
        scores_ready = sem("scores_ready")
        negmax_ready = sem("negmax_ready")
        rowsum_ready = sem("rowsum_ready")
        logsum_ready = sem("logsum_ready")
        shift_full = sem("shift_full")
        shift_cut = sem("shift_cut")
        shift_ready = sem("shift_ready")
        row_ready = sem("row_ready")
        row_put = sem("row_put")
        v_ready = sem("v_ready")
        v_cut = sem("v_cut")
        v_split = sem("v_split")
        st_ready = sem("st_ready")
        exp_done = sem("exp_done")
        w_cut_act = sem("w_cut_act")
        w_cut_dve = sem("w_cut_dve")
        w_split_pool = sem("w_split_pool")
        w_split_dve = sem("w_split_dve")
        av_done = sem("av_done")
        acc0_ready = sem("acc0_ready")
        acc_read = sem("acc_read")
        out_sent = [sem("out_sent0"), sem("out_sent1")]
        sp_passed = sem("sp_passed")
        pool_passed = sem("pool_passed")
        act_passed = sem("act_passed")

        PRE = RING

        def cols(h):
            return slice(h * HALF, (h + 1) * HALF)

        def front(s, more):
            what, k, image = (FRONT | ROWS).get(s, (None, 0, 0))
            return (what, k, image) if image == 0 or more else (None, 0, 0)

        def place(s, b):
            return b + s // PER, s % PER // JT, s % JT

        def quarter(i):
            return slice(i * QUARTER, (i + 1) * QUARTER)

        def flat(banks):
            return banks[:, :, :].rearrange("p i n -> p (i n)")

        FIRST_HOME = {0: flat(acc), 1: slot[0][:, :], 2: flat(st), 3: flat(acc), 4: slot[1][:, :], 5: slot[0][:, :]}

        def s_home(t, first):
            return FIRST_HOME[t] if first else slot[SLOT[S, t]][:, :]

        def v_home(i, first):
            if first:
                return (slot[1][:, cols(1)], slot[0][:, cols(0)], st[:, 1, :], acc[:, 0, :])[i]
            return slot[SLOT[V, i // 2]][:, cols(i % 2)]

        def made(mine, b, tile):
            return len(mine) * (b + tile // PER) + sum(j <= tile % PER for j in mine)

        def last_ring(mine):
            return sum(j >= PER - RING for j in mine)

        CUT_BY_DVE = [j for j in range(PER) if j not in CUT_BY_ACT]
        SPLIT_BY_DVE = [j for j in range(PER) if j not in SPLIT_BY_POOL]

        def wait_w_cut(engine, b, tile):
            if tile % PER in CUT_BY_ACT:
                engine.wait_ge(w_cut_act, made(CUT_BY_ACT, b, tile))
            else:
                engine.wait_ge(w_cut_dve, made(CUT_BY_DVE, b, tile))

        def wait_w_split(engine, b, tile):
            if tile % PER in SPLIT_BY_POOL:
                engine.wait_ge(w_split_pool, last_ring(SPLIT_BY_POOL) + made(SPLIT_BY_POOL, b, tile))
            else:
                engine.wait_ge(w_split_dve, last_ring(SPLIT_BY_DVE) + made(SPLIT_BY_DVE, b, tile))

        block = ctx.enter_context(nc.Block())

        @block.sync
        def _(sp):
            for h in range(2):
                sp.sem_inc(out_sent[h], 1)
            sp.dma_start(wqk[:, :, :], wqk_t.rearrange("(t p) m -> p t m", p=P)).then_inc(wqk_in, DMA)
            for i in range(4):
                sp.dma_start(x_sb[:, 0, :, quarter(i)], x_v[0, :, :, quarter(i)]).then_inc(x0_in[i], DMA)
            sp.dma_start(wv[:, :, :], wv_t.rearrange("(t p) m -> p t m", p=P)).then_inc(wv_in, DMA)

            def wait(done, count):
                sp.wait_ge(done, count)
                sp.sem_inc(sp_passed, 1)

            def blocks(dst, row, src_row, n, h, done):
                sp.dma_start(dst[row * CQK:(row + n) * CQK, cols(h)].bitcast(fp32),
                             qk_parts[src_row * CQK:(src_row + n) * CQK, cols(h)].bitcast(fp32)).then_inc(done, DMA)

            def first_stacks(b):
                wait(scores_ready, JT * b)
                for h in range(2):
                    wait(kb_in[h], DMA * b)
                    wait(qb_in[h], DMA * b)
                for h in range(2):
                    wait(qk_split, 2 * b + h - 1)
                    blocks(k_a, 0, 2, 1, h, ka_in[h])
                    blocks(k_a, 1, 2, 2, h, ka_in[h])
                    blocks(q_a, 0, 0, 2, h, qa_in[h])
                    blocks(q_a, 2, 0, 1, h, qa_in[h])

            def second_stack(dst, src, h, done):
                sp.dma_start(dst[0:SHIFT, cols(h)].bitcast(fp32), src[0:SHIFT, cols(h)].bitcast(fp32)).then_inc(done, DMA)

            for h in range(2):
                sp.wait_ge(k_lo_put, h + 1)
                sp.wait_ge(k_hi_put, h + 1)
                second_stack(k_b, k_a, h, kb_in[h])
                sp.wait_ge(q_put, h + 1)
                sp.wait_ge(q_hi_put[h], 1)
                second_stack(q_b, q_a, h, qb_in[h])
            for b in range(1, BATCH):
                sp.dma_start(x_sb[:, b, :, :], x_v[b]).then_inc(x_in, DMA)
                sp.wait_ge(x_in, DMA * b)

            def send(b, h):
                wait(acc_read, 2 * (2 * b + h) + 4)
                sp.dma_start(out_v[b, :, :, cols(h)], o_sb[:, h, :, :]).then_inc(out_sent[h], DMA)

            with sp.Fori(0, BATCH - 1) as b:
                first_stacks(b + 1)
                wait(st_ready, PER * b + JT)
                wait(qa_in[0], 2 * DMA * (b + 1))
                second_stack(q_b, q_a, 0, qb_in[0])
                send(b, 0)
                wait(st_ready, PER * b + JT + TH)
                wait(ka_in[0], 2 * DMA * (b + 1))
                second_stack(k_b, k_a, 0, kb_in[0])
                wait(st_ready, PER * b + PER)
                wait(ka_in[1], 2 * DMA * (b + 1))
                second_stack(k_b, k_a, 1, kb_in[1])
                wait(qa_in[1], 2 * DMA * (b + 1))
                second_stack(q_b, q_a, 1, qb_in[1])
                send(b, 1)
            send(BATCH - 1, 0)
            for c in range(CT):
                sp.wait_ge(acc_read, 4 * BATCH + 1 + c)
                sp.dma_start(out_v[BATCH - 1, :, c, cols(1)], o_sb[:, 1, c, :]).then_inc(out_sent[1], DMA)
            for h in range(2):
                sp.wait_ge(out_sent[h], DMA * (BATCH + h) + 1)

        @block.gpsimd
        def _(pool):
            if last_ring(SPLIT_BY_POOL):
                pool.sem_inc(w_split_pool, last_ring(SPLIT_BY_POOL))
            pool.dma_start(bias[:, :], bias_qk).then_inc(bias_in, DMA)
            nc.gpsimd.memset(eye[:, :], 0.0).then_inc(eye_made, 1)
            pool.wait_ge(eye_made, 1)
            nc.gpsimd.affine_select(out=eye[:, :], in_=eye[:, :], compare_op=ALU.not_equal, fill=1.0,
                                    base=0, pattern=[[-1, P]], channel_multiplier=1).then_inc(eye_made, 1)
            pool.wait_ge(wcut, 2)
            nc.gpsimd.tensor_tensor(wv_lo[:, :, :], wv[:, :, :], wv_hi[:, :, :].bitcast(fp32),
                                    ALU.subtract).then_inc(wv_split, 1)
            pool.dma_start(bv_sb[:, :], bv).then_inc(bv_in, DMA)

            def split_w(b, tile):
                if tile % PER not in SPLIT_BY_POOL:
                    return
                n, j = PER * b + tile, tile % JT
                pool.wait_ge(exp_done, n + 1)
                wait_w_cut(pool, b, tile)
                pool.wait_ge(av_done, n + 1)
                nc.gpsimd.tensor_tensor(w_lo[:, j % RING, :], w_full[:, j % RING, :],
                                        w_hi[:, j % RING, :].bitcast(fp32), ALU.subtract).then_inc(w_split_pool, 1)

            for j in range(AHEAD):
                split_w(0, j)

            with pool.Fori(0, BATCH - 1) as b:
                for h in range(2):
                    pool.wait_ge(x_cut, 2 * b + h + 5)
                    pool.sem_inc(pool_passed, 1)
                    nc.gpsimd.tensor_tensor(x_lo[:, :, cols(h)], x_sb[:, b + 1, :, cols(h)],
                                            x_hi[:, :, cols(h)].bitcast(fp32), ALU.subtract).then_inc(x_split, 1)
                for s in range(PER):
                    split_w(b, s + AHEAD)
            for s in range(PER - AHEAD):
                split_w(BATCH - 1, s + AHEAD)

        @block.scalar
        def _(act):
            act.preload_act_table_set("natural_log_exp_and_others")
            act.wait_ge(consts, 2)
            nc.scalar.activation(k_b[SHIFT:K_B, :], ones[SHIFT:K_B, :], ACT.Copy).then_inc(ones_put, 1)
            act.wait_ge(wqk_in, DMA)
            nc.scalar.activation(wqk_hi[:, :, :], wqk[:, :, :], ACT.Copy).then_inc(wcut, 1)
            for i in range(4):
                act.wait_ge(x0_in[i], DMA)
                nc.scalar.activation(x_hi[:, :, quarter(i)], x_sb[:, 0, :, quarter(i)], ACT.Copy).then_inc(x_cut, 1)

            def cut_qk(b, h, low=LOW):
                act.wait_ge(qk_ready, 2 * b + h + 1)
                nc.scalar.activation(qk_cut[:, cols(h)], slot[SLOT[QK, h]][:, 0:HALF], ACT.Identity,
                                     bias=lo_bias[:, low:low + 1],
                                     scale=lo_rows[:, low:low + 1]).then_inc(qk_cut_done, 1)

            def sum_exp(b, t, first=False):
                act.wait_ge(negmax_ready, JT * b + t + 1)
                if first and t in (2, 3):
                    act.wait_ge(rowsum_ready, t - 1)
                nc.scalar.activation(dump[:, t % 2, :], s_home(t, first), ACT.Exp,
                                     bias=negmax[:, t:t + 1], accum_out=rowsum[:, t:t + 1]).then_inc(rowsum_ready, 1)

            def log_sums(b, h):
                act.wait_ge(rowsum_ready, JT * b + TH * h + TH)
                nc.scalar.activation(logsum[:, TH * h:TH * h + TH], rowsum[:, TH * h:TH * h + TH],
                                     ACT.Ln).then_inc(logsum_ready, 1)

            def put_rows(b, h):
                act.wait_ge(row_ready, 2 * b + h + 1)
                nc.scalar.activation(q_b[SHIFT:K_B, cols(h)], st[0:2, 0, :], ACT.Copy).then_inc(row_put, 1)

            def cut_v(b, i, first=False):
                act.wait_ge(v_ready, 4 * b + i + 1)
                if not first:
                    act.wait_ge(av_done, PRE + PER * (b - 1) + JT + VT * i + VT)
                nc.scalar.activation(v_hi[:, VT * i:VT * i + VT, :],
                                     v_home(i, first).rearrange("p (j c) -> p j c", c=C), ACT.Copy).then_inc(v_cut, 1)

            def exp(b, tile):
                n, j = PER * b + tile, tile % JT
                act.wait_ge(st_ready, n + 1)
                if tile % PER in CUT_BY_ACT:
                    act.wait_ge(av_done, n + 1)
                    nc.scalar.activation(w_hi[:, j % RING, :], st[:, j % 2, :], ACT.Exp).then_inc(w_cut_act, 1)
                wait_w_split(act, b, tile - RING)
                nc.scalar.activation(w_full[:, j % RING, :], st[:, j % 2, :], ACT.Exp).then_inc(exp_done, 1)

            def cut_x(b, h):
                if h == 0:
                    act.wait_ge(x_in, DMA * b)
                    act.wait_ge(v_ready, 4 * b)
                    act.sem_inc(act_passed, 1)
                nc.scalar.activation(x_hi[:, :, cols(h)], x_sb[:, b, :, cols(h)], ACT.Copy).then_inc(x_cut, 1)

            def put_k_hi(h):
                act.wait_ge(qk_cut_done, h + 1)
                nc.scalar.activation(k_a[0:2 * CQK, cols(h)], qk_cut[2 * CQK:4 * CQK, cols(h)].bitcast(fp32),
                                     ACT.Copy).then_inc(k_hi_put, 1)

            act.wait_ge(wsplit, 2)
            cut_qk(0, 0, FIRST_LOW)
            put_k_hi(0)
            cut_qk(0, 1, FIRST_LOW)
            act.wait_ge(q_put, 1)
            nc.scalar.activation(q_a[2 * CQK:3 * CQK, cols(0)], q_a[0:CQK, cols(0)].bitcast(fp32),
                                 ACT.Copy).then_inc(q_hi_put[0], 1)
            put_k_hi(1)
            act.wait_ge(wv_in, DMA)
            nc.scalar.activation(wv_hi[:, :, :], wv[:, :, :], ACT.Copy).then_inc(wcut, 1)
            act.wait_ge(eye_made, 2)
            nc.scalar.activation(eye_r[:, :], eye[:, :], ACT.Copy).then_inc(wcut, 1)
            for t in range(TH):
                sum_exp(0, t, True)
            log_sums(0, 0)
            cut_v(0, 0, True)
            cut_v(0, 1, True)
            put_rows(0, 0)
            cut_v(0, 2, True)
            cut_v(0, 3, True)
            exp(0, 0)
            sum_exp(0, TH, True)
            exp(0, 1)
            sum_exp(0, TH + 1, True)

            def turn(b, more):
                for s in range(PER):
                    if s + AHEAD < PER or more:
                        exp(b, s + AHEAD)
                    if more and s < 2:
                        cut_x(b + 1, s)
                    what, k, image = front(s, more)
                    if what == ROW:
                        put_rows(b + image, k)
                    what, t, image = front(s - 1, more)
                    if what == S:
                        sum_exp(b + image, t)
                        if t % TH == TH - 1:
                            log_sums(b + image, t // TH)
                    what, k, image = front(s, more)
                    if what == QK:
                        cut_qk(b + 1, k)
                    if what == V:
                        for i in (2 * k, 2 * k + 1):
                            cut_v(b + 1, i)

            with act.Fori(0, BATCH - 1) as b:
                turn(b, True)
            turn(BATCH - 1, False)

        @block.vector
        def _(dve):
            dve.sem_inc(w_split_dve, last_ring(SPLIT_BY_DVE))
            nc.vector.memset(idle[:, :], 0.0).then_inc(consts, 1)
            nc.vector.memset(ones[SHIFT:SHIFT + 32, :], 1.0).then_inc(consts, 1)
            for low, blocks in LOW_BLOCKS.items():
                for row in range(4):
                    nc.vector.memset(lo_rows[row * CQK:(row + 1) * CQK, low:low + 1],
                                     float(row in blocks)).then_inc(consts, 1)
            dve.wait_ge(wcut, 1)
            nc.vector.tensor_tensor(wqk_lo[:, :, :], wqk[:, :, :], wqk_hi[:, :, :].bitcast(fp32),
                                    ALU.subtract).then_inc(wsplit, 1)
            dve.wait_ge(bias_in, DMA)
            dve.wait_ge(consts, 10)
            nc.vector.tensor_scalar(lo_bias[:, :], lo_rows[:, :], bias[:, :], None, ALU.mult).then_inc(wsplit, 1)
            for i in range(4):
                dve.wait_ge(x_cut, i + 1)
                nc.vector.tensor_tensor(x_lo[:, :, quarter(i)], x_sb[:, 0, :, quarter(i)],
                                        x_hi[:, :, quarter(i)].bitcast(fp32), ALU.subtract).then_inc(x0_split, 1)

            def split_block(dst, h, rows):
                return nc.vector.scalar_tensor_tensor(
                    out=dst, in0=slot[SLOT[QK, h]][rows, 0:HALF], scalar=bias[rows, 0:1],
                    in1=qk_cut[rows, cols(h)].bitcast(fp32), op0=ALU.add, op1=ALU.subtract)

            def put_k_lo(h):
                dve.wait_ge(qk_cut_done, h + 1)
                split_block(k_a[2 * CQK:3 * CQK, cols(h)], h, slice(3 * CQK, 4 * CQK)).then_inc(k_lo_put, 1)

            def put_q(h):
                dve.wait_ge(qk_cut_done, h + 1)
                split_block(q_a[0:2 * CQK, cols(h)], h, slice(0, 2 * CQK)).then_inc(q_put, 1)

            def split_qk(b, h):
                dve.wait_ge(qk_cut_done, 2 * b + h + 1)
                dve.wait_ge(qb_in[h], DMA * b)
                dve.wait_ge(kb_in[h], DMA * b)
                split_block(qk_parts[:, cols(h)], h, slice(0, P)).then_inc(qk_split, 1)

            def row_max(b, t, first=False):
                dve.wait_ge(scores_ready, JT * b + t + 1)
                nc.vector.tensor_reduce(out=negmax[:, t:t + 1], in_=s_home(t, first),
                                        op=ALU.max, axis=AX.X, negate=True).then_inc(negmax_ready, 1)

            def shifts(b, h):
                part = slice(TH * h, TH * h + TH)
                dve.wait_ge(logsum_ready, 2 * b + h + 1)
                nc.vector.tensor_tensor(shift[:, part], negmax[:, part], logsum[:, part],
                                        ALU.subtract).then_inc(shift_full, 1)
                dve.wait_ge(shift_full, 2 * b + h + 1)
                nc.vector.tensor_copy(shift_parts[:, part, HI], shift[:, part]).then_inc(shift_cut, 1)
                dve.wait_ge(shift_cut, 2 * b + h + 1)
                nc.vector.tensor_tensor(shift_parts[:, part, LO], shift[:, part],
                                        shift_parts[:, part, HI].bitcast(fp32), ALU.subtract).then_inc(shift_ready, 1)

            def split_v(b, i, first=False):
                dve.wait_ge(v_cut, 4 * b + i + 1)
                nc.vector.tensor_tensor(v_lo[:, VT * i:VT * i + VT, :],
                                        v_home(i, first).rearrange("p (j c) -> p j c", c=C),
                                        v_hi[:, VT * i:VT * i + VT, :].bitcast(fp32), ALU.subtract).then_inc(v_split, 1)

            def cut_w(b, tile):
                if tile % PER in CUT_BY_ACT:
                    return
                n, j = PER * b + tile, tile % JT
                dve.wait_ge(exp_done, n + 1)
                dve.wait_ge(av_done, n + 1)
                nc.vector.tensor_copy(w_hi[:, j % RING, :], w_full[:, j % RING, :]).then_inc(w_cut_dve, 1)

            def split_w(b, tile):
                if tile % PER in SPLIT_BY_POOL:
                    return
                n, j = PER * b + tile, tile % JT
                dve.wait_ge(exp_done, n + 1)
                wait_w_cut(dve, b, tile)
                dve.wait_ge(av_done, n + 1)
                nc.vector.tensor_tensor(w_lo[:, j % RING, :], w_full[:, j % RING, :],
                                        w_hi[:, j % RING, :].bitcast(fp32), ALU.subtract).then_inc(w_split_dve, 1)

            def finish(b, h, c):
                if c == 0:
                    dve.wait_ge(acc0_ready, 2 * b + h + 1)
                    dve.wait_ge(out_sent[h], DMA * b + 1)
                else:
                    dve.wait_ge(av_done, PRE + PER * b + JT * h + JT)
                nc.vector.scalar_tensor_tensor(out=o_sb[:, h, c, :], in0=acc[:, c, :], scalar=bv_sb[:, c:c + 1],
                                               in1=x_sb[:, b, c, cols(h)], op0=ALU.add, op1=ALU.add).then_inc(acc_read, 1)

            put_q(0)
            put_k_lo(0)
            put_k_lo(1)
            for t in range(TH):
                row_max(0, t, True)
            put_q(1)
            dve.wait_ge(q_put, 2)
            nc.vector.tensor_copy(q_a[2 * CQK:3 * CQK, cols(1)],
                                  q_a[0:CQK, cols(1)].bitcast(fp32)).then_inc(q_hi_put[1], 1)
            shifts(0, 0)
            for i in range(4):
                split_v(0, i, True)
                if i == 1:
                    row_max(0, TH, True)
            row_max(0, TH + 1, True)
            dve.wait_ge(bv_in, DMA)
            for j in range(AHEAD):
                cut_w(0, j)
                split_w(0, j)

            def turn(b, more):
                for s in range(PER):
                    what, k, image = front(s - 1, more)
                    before, t, its = front(s - 2, more)
                    summed = before == S and t % TH == TH - 1
                    if summed:
                        shifts(b + its, t // TH)
                    ahead = s + AHEAD < PER or more
                    if s % JT == JT - 1:
                        for c in range(CT):
                            finish(b, s // JT, c)
                    if ahead:
                        cut_w(b, s + AHEAD)
                    if what == QK:
                        split_qk(b + 1, k)
                    if ahead:
                        split_w(b, s + AHEAD)
                    if what == V:
                        for i in (2 * k, 2 * k + 1):
                            split_v(b + 1, i)
                    what, k, image = front(s, more)
                    if what == S:
                        row_max(b + image, k)
                    if s == PER - 1 and more:
                        for i in (2, 3):
                            split_v(b + 1, i)

            with dve.Fori(0, BATCH - 1) as b:
                turn(b, True)
            turn(BATCH - 1, False)

        @block.tensor
        def _(pe):
            pe.sem_inc(av_done, PRE)
            pe.sem_inc(acc_read, 2)

            def group(dst, terms):
                for i, (lhs, rhs) in enumerate(terms):
                    last = nc.tensor.matmul(dst, lhs, rhs, start=(i == 0), stop=(i == len(terms) - 1))
                return last

            def project_qk(b, h):
                pe.wait_ge(x_split, 2 * b + h - 1)
                pe.wait_ge(rowsum_ready, JT * b - 1 + h)
                terms = [(w[:, c, :], xs[:, c, cols(h)]) for c in range(CT)
                         for w, xs in ((wqk_hi, x_hi), (wqk_lo, x_hi), (wqk_hi, x_lo))]
                group(slot[SLOT[QK, h]][:, 0:HALF], terms).then_inc(qk_ready, 1)

            def first_project_qk(i):
                x = quarter(i)
                dst = slot[SLOT[QK, i // 2]][:, i % 2 * QUARTER:(i % 2 + 1) * QUARTER]
                if i == 0:
                    pe.wait_ge(wcut, 1)
                pe.wait_ge(x_cut, i + 1)
                for c in range(CT):
                    nc.tensor.matmul(dst, wqk_hi[:, c, :], x_hi[:, c, x], start=(c == 0), stop=False)
                if i == 0:
                    pe.wait_ge(wsplit, 1)
                for c in range(CT):
                    nc.tensor.matmul(dst, wqk_lo[:, c, :], x_hi[:, c, x], start=False, stop=False)
                pe.wait_ge(x0_split, i + 1)
                for c in range(CT):
                    last = nc.tensor.matmul(dst, wqk_hi[:, c, :], x_lo[:, c, x], start=False, stop=(c == CT - 1))
                if i % 2 == 1:
                    last.then_inc(qk_ready, 1)

            def scores(b, t):
                if t == 0:
                    pe.wait_ge(qa_in[0], 2 * DMA * b)
                    pe.wait_ge(ka_in[0], 2 * DMA * b)
                    pe.wait_ge(ka_in[1], 2 * DMA * b)
                elif t in (2, 3):
                    pe.wait_ge(rowsum_ready, JT * b + t - 1)
                elif t in (4, 6):
                    pe.wait_ge(rowsum_ready, JT * b + t)
                if t == TH:
                    pe.wait_ge(qa_in[1], 2 * DMA * b)
                if t in (5, 7):
                    pe.wait_ge(v_split, 4 * b + t - 3)
                for h in range(2):
                    last = nc.tensor.matmul(s_home(t, False)[:, cols(h)], q_a[0:K_A, t * P:(t + 1) * P],
                                            k_a[0:K_A, cols(h)], start=True, stop=True)
                last.then_inc(scores_ready, 1)

            def first_scores(t):
                for h in range(2):
                    if t == 0:
                        pe.wait_ge(k_lo_put, h + 1)
                        pe.wait_ge(k_hi_put, h + 1)
                    if t == 0 and h == 0:
                        pe.wait_ge(q_put, 1)
                        pe.wait_ge(q_hi_put[0], 1)
                    if t == 3 and h == 0:
                        pe.wait_ge(rowsum_ready, 1)
                    if t == 4 and h == 0:
                        pe.wait_ge(q_put, 2)
                        pe.wait_ge(q_hi_put[1], 1)
                    if t in (4, 5) and h == 0:
                        pe.wait_ge(v_split, t - 3)
                    last = nc.tensor.matmul(s_home(t, True)[:, cols(h)], q_a[0:K_A, t * P:(t + 1) * P],
                                            k_a[0:K_A, cols(h)], start=True, stop=True)
                last.then_inc(scores_ready, 1)

            def v_tile(t, first=False):
                px = slice(t * P, (t + 1) * P)
                terms = [(xs[:, c, px], w[:, c, :]) for c in range(CT)
                         for xs, w in ((x_hi, wv_hi), (x_hi, wv_lo), (x_lo, wv_hi))]
                last = group(v_home(t // VT, first)[:, t % VT * C:(t % VT + 1) * C], terms)
                if t % VT == VT - 1:
                    last.then_inc(v_ready, 1)

            def project_v(b, g):
                pe.wait_ge(rowsum_ready, JT * b + 3 + 2 * g)
                for jj in range(TH):
                    v_tile(TH * g + jj)

            def rows(b, h, first=False):
                pe.wait_ge(shift_ready, 2 * b + h + 1)
                if first:
                    pe.wait_ge(wcut, 3)
                    pe.wait_ge(ones_put, 1)
                    pe.wait_ge(rowsum_ready, 3)
                else:
                    pe.wait_ge(exp_done, PER * b + JT * h - 1)
                for t in range(TH):
                    last = nc.tensor.matmul(st[0:2, 0, t * P:(t + 1) * P], shift_parts[:, TH * h + t, :],
                                            eye_r[:, :], start=True, stop=True)
                last.then_inc(row_ready, 1)

            def scores_t(b, h, j):
                if j == 0:
                    pe.wait_ge(row_put, 2 * b + h + 1)
                    pe.wait_ge(qb_in[h], DMA * (b + 1))
                    if h == 0:
                        pe.wait_ge(kb_in[0], DMA * (b + 1))
                if j == TH and h == 0:
                    pe.wait_ge(kb_in[1], DMA * (b + 1))
                nc.tensor.matmul(st[:, j % 2, :], k_b[0:K_B, j * P:(j + 1) * P], q_b[0:K_B, cols(h)],
                                 start=True, stop=True).then_inc(st_ready, 1)

            def weigh_v(b, h, j):
                n = PER * b + JT * h + j
                r = j % RING
                if h == 0 and j in (0, TH):
                    pe.wait_ge(v_split, 4 * b + 2 + j // VT)
                wait_w_cut(pe, b, JT * h + j)
                for c in range(CT):
                    ch = slice(c * P, (c + 1) * P)
                    if j == 0:
                        pe.wait_ge(acc_read, 2 * (2 * b + h) + c + 1)
                    for v in (v_hi, v_lo):
                        nc.tensor.matmul(acc[:, c, :], v[:, j, ch], w_hi[:, r, :],
                                         start=(j == 0 and v is v_hi), stop=False)
                    if j == JT - 1 and c == 0:
                        wait_w_split(pe, b, JT * h + j)
                        nc.tensor.matmul(acc[:, c, :], v_hi[:, j, ch], w_lo[:, r, :],
                                         start=False, stop=True).then_inc(acc0_ready, 1)
                wait_w_split(pe, b, JT * h + j)
                for c in range(1 if j == JT - 1 else 0, CT):
                    last = nc.tensor.matmul(acc[:, c, :], v_hi[:, j, c * P:(c + 1) * P], w_lo[:, r, :],
                                            start=False, stop=(j == JT - 1))
                last.then_inc(av_done, 1)

            def keep_busy(count):
                for i in range(count):
                    nc.tensor.matmul(st[:, 0, :], idle[:, 0:P], idle[:, :], start=True, stop=True)

            pe.wait_ge(consts, 1)
            keep_busy(LOAD_PRODUCTS)
            for i in range(4):
                first_project_qk(i)
            keep_busy(WAIT_PRODUCTS)
            for t in range(3):
                first_scores(t)
            pe.wait_ge(wv_split, 1)
            for t in range(2):
                v_tile(t, True)
            first_scores(3)
            pe.wait_ge(rowsum_ready, 2)
            for t in range(2, 4):
                v_tile(t, True)
            pe.wait_ge(rowsum_ready, 3)
            for t in range(4, 6):
                v_tile(t, True)
            pe.wait_ge(rowsum_ready, 4)
            v_tile(6, True)
            rows(0, 0, True)
            first_scores(TH)
            v_tile(7, True)
            scores_t(0, 0, 0)
            first_scores(TH + 1)
            pe.wait_ge(v_split, 3)
            scores_t(0, 0, 1)
            pe.wait_ge(v_split, 4)

            def turn(b, more):
                for s in range(PER):
                    if s + AHEAD < PER or more:
                        pe.wait_ge(exp_done, PER * b + s + AHEAD - 1)
                        scores_t(*place(s + AHEAD, b))
                    what, k, image = front(s, more)
                    if what == ROW:
                        rows(b + image, k)
                    weigh_v(b, s // JT, s % JT)
                    if what == S:
                        scores(b + image, k)
                    elif what == QK:
                        project_qk(b + 1, k)
                    elif what == V:
                        project_v(b + 1, k)

            with pe.Fori(0, BATCH - 1) as b:
                turn(b, True)
            turn(BATCH - 1, False)


_OUT = (4, 256, 32, 32)


def kernel(x, L0_conv_Wq, L0_conv_bq, L0_conv_Wk, L0_conv_bk, L0_conv_Wv, L0_conv_bv):
    import numpy as np
    import concourse.bacc as bacc
    from concourse.bass_utils import run_bass_kernel_spmd

    x, wq, bq, wk, bk, wv, bv = (np.asarray(a) for a in (
        x, L0_conv_Wq, L0_conv_bq, L0_conv_Wk, L0_conv_bk, L0_conv_Wv, L0_conv_bv))
    images, channels = x.shape[:2]
    arrays = {
        "x": np.ascontiguousarray(x.reshape(images, channels, -1)),
        "wqk_t": np.ascontiguousarray(np.concatenate([wq, wq, wk, wk], axis=0).T),
        "bias_qk": np.ascontiguousarray(np.concatenate([bq, bq, bk, bk])[:, None]),
        "wv_t": np.ascontiguousarray(wv.T),
        "bv": np.ascontiguousarray(bv.reshape(-1, 128).T),
    }
    nc = bacc.Bacc("TRN2", target_bir_lowering=False, num_devices=1)
    args = [nc.dram_tensor(n, a.shape, mybir.dt.from_np(a.dtype), kind="ExternalInput").ap() for n, a in arrays.items()]
    out = nc.dram_tensor("out", arrays["x"].shape, mybir.dt.float32, kind="ExternalOutput").ap()
    nonlocal_attention(nc, *args, out)
    r = run_bass_kernel_spmd(nc, [arrays], core_ids=[0])
    return r.results[0]["out"].reshape(x.shape)
```
